# Optimizing a Trainium2 kernel written in Bass

```python
import numpy as np
import jax
import jax.numpy as jnp

def _softmax(x, axis=-1):
    return jax.nn.softmax(x, axis=axis)

def _gelu(x):
    return jax.nn.gelu(x, approximate=True)

def _silu(x):
    return jax.nn.silu(x)

def _sigmoid(x):
    return jax.nn.sigmoid(x)

def _layernorm(x, axis=-1, eps=1e-05):
    m = jnp.mean(x, axis=axis, keepdims=True)
    v = jnp.var(x, axis=axis, keepdims=True)
    return (x - m) / jnp.sqrt(v + eps)

def _scatter_add(tgt, idx, src, axis=0):
    return tgt.at[idx].add(src)

def _segment_sum(src, seg, n):
    return jax.ops.segment_sum(src, seg, n)
kernel_name = 'mk_gnn_resnorm_d2_gnn_r8_a61ec8'

def setup_inputs(seed: int=0):
    np.random.seed(seed)
    _w = jnp.asarray

    def _rec_inputs():
        import jax
        import jax.numpy as jnp
        _gk = jax.random.key(seed)
        x = -0.0005963 + 1.001 * jax.random.normal(jax.random.fold_in(_gk, 1), (384, 1024), jnp.float32)
        _s = jax.random.randint(jax.random.fold_in(_gk, 2), (3072,), 0, 384, jnp.int32)
        _d = jax.random.randint(jax.random.fold_in(_gk, 3), (3072,), 0, 384, jnp.int32)
        _loop = jnp.arange(384, dtype=jnp.int32)
        src = jnp.concatenate([_s, _d, _loop])
        dst = jnp.concatenate([_d, _s, _loop])
        _o = jnp.argsort(dst, stable=True)
        src = src[_o]
        dst = dst[_o]
        edge_type_5 = jax.random.randint(jax.random.fold_in(_gk, 12), (6528,), 0, 5, jnp.int32)
        return (x, src, dst, edge_type_5)
    x, src, dst, edge_type_5 = _rec_inputs()

    def _L0_gnn_setup():
        import jax, jax.numpy as jnp
        import numpy as np
        N = 384
        E = 12288
        IN_F = 1024
        OUT_F = 1024
        H = 16
        D = OUT_F // H
        NUM_ETYPES = 4

        def _build_mask(edge_index, edge_type, edge_type_weights, dtype):
            src, dst = (edge_index[0], edge_index[1])
            w = jax.nn.softplus(edge_type_weights)
            mask = jnp.full((N, N), -jnp.inf, dtype=dtype)
            mask = mask.at[src, dst].set(w[edge_type - 1])
            diag = jnp.diagonal(mask)
            idx = jnp.arange(N)
            mask = mask.at[idx, idx].set(jnp.where(jnp.isneginf(diag), w[3], diag))
            return mask
        key = jax.random.key(seed)
        ks = jax.random.split(key, 20)
        p = lambda k, shape: jax.random.normal(k, shape, dtype=jnp.float32) * 0.02
        return {'x': jax.random.normal(ks[0], (N, IN_F), dtype=jnp.float32), 'edge_index': jax.random.randint(ks[1], (2, E), 0, N), 'edge_type': jax.random.randint(ks[2], (E,), 1, NUM_ETYPES + 1), 'edge_type_weights': jnp.ones((NUM_ETYPES,), jnp.float32) + 0.1 * jax.random.normal(ks[3], (NUM_ETYPES,), dtype=jnp.float32), 'wq': p(ks[4], (OUT_F, IN_F)), 'bq': p(ks[5], (OUT_F,)), 'wk': p(ks[6], (OUT_F, IN_F)), 'bk': p(ks[7], (OUT_F,)), 'wv': p(ks[8], (OUT_F, IN_F)), 'bv': p(ks[9], (OUT_F,)), 'wiq': p(ks[10], (OUT_F, OUT_F)), 'biq': p(ks[11], (OUT_F,)), 'wik': p(ks[12], (OUT_F, OUT_F)), 'bik': p(ks[13], (OUT_F,)), 'wiv': p(ks[14], (OUT_F, OUT_F)), 'biv': p(ks[15], (OUT_F,)), 'wo': p(ks[16], (OUT_F, OUT_F)), 'bo': p(ks[17], (OUT_F,))}
    _L0_gnn_all = _L0_gnn_setup()
    _L0_gnn_in = {k: v for k, v in _L0_gnn_all.items() if k in ('edge_type_weights', 'wq', 'bq', 'wk', 'bk', 'wv', 'bv', 'wiq', 'biq', 'wik', 'bik', 'wiv', 'biv', 'wo', 'bo')}
    del _L0_gnn_all

    def _L1_gnn_setup():
        import jax, jax.numpy as jnp
        import numpy as np
        N = 2500
        E = 40000
        IN = 1024
        HID = 256
        H = 4
        D = HID // H
        OUT = 1024
        EPS = 1e-06
        NEG_SLOPE = 0.2
        key = jax.random.key(seed)
        ks = jax.random.split(key, 8)
        x = jax.random.normal(ks[0], (N, IN), dtype=jnp.float32)
        edge_index = jax.random.randint(ks[1], (2, E), 0, N, dtype=jnp.int64)
        s = 0.02
        return {'x': x, 'edge_index': edge_index, 'rms_w': jnp.ones((IN,), dtype=jnp.float32), 'W_down': jax.random.normal(ks[2], (IN, HID), dtype=jnp.float32) * s, 'Wl': jax.random.normal(ks[3], (HID, HID), dtype=jnp.float32) * s, 'Wr': jax.random.normal(ks[4], (HID, HID), dtype=jnp.float32) * s, 'att': jax.random.normal(ks[5], (H, D), dtype=jnp.float32) * s, 'W_up': jax.random.normal(ks[6], (HID, OUT), dtype=jnp.float32) * s}
    _L1_gnn_all = _L1_gnn_setup()
    _L1_gnn_in = {k: v for k, v in _L1_gnn_all.items() if k in ('rms_w', 'W_down', 'Wl', 'Wr', 'att', 'W_up')}
    del _L1_gnn_all
    return {'x': x, 'src': src, 'dst': dst, 'edge_type_5': edge_type_5, 'L0_gnn_edge_type_weights': _L0_gnn_in['edge_type_weights'], 'L0_gnn_wq': _L0_gnn_in['wq'], 'L0_gnn_bq': _L0_gnn_in['bq'], 'L0_gnn_wk': _L0_gnn_in['wk'], 'L0_gnn_bk': _L0_gnn_in['bk'], 'L0_gnn_wv': _L0_gnn_in['wv'], 'L0_gnn_bv': _L0_gnn_in['bv'], 'L0_gnn_wiq': _L0_gnn_in['wiq'], 'L0_gnn_biq': _L0_gnn_in['biq'], 'L0_gnn_wik': _L0_gnn_in['wik'], 'L0_gnn_bik': _L0_gnn_in['bik'], 'L0_gnn_wiv': _L0_gnn_in['wiv'], 'L0_gnn_biv': _L0_gnn_in['biv'], 'L0_gnn_wo': _L0_gnn_in['wo'], 'L0_gnn_bo': _L0_gnn_in['bo'], 'L1_gnn_rms_w': _L1_gnn_in['rms_w'], 'L1_gnn_W_down': _L1_gnn_in['W_down'], 'L1_gnn_Wl': _L1_gnn_in['Wl'], 'L1_gnn_Wr': _L1_gnn_in['Wr'], 'L1_gnn_att': _L1_gnn_in['att'], 'L1_gnn_W_up': _L1_gnn_in['W_up']}

def reference(x, src, dst, edge_type_5, L0_gnn_edge_type_weights, L0_gnn_wq, L0_gnn_bq, L0_gnn_wk, L0_gnn_bk, L0_gnn_wv, L0_gnn_bv, L0_gnn_wiq, L0_gnn_biq, L0_gnn_wik, L0_gnn_bik, L0_gnn_wiv, L0_gnn_biv, L0_gnn_wo, L0_gnn_bo, L1_gnn_rms_w, L1_gnn_W_down, L1_gnn_Wl, L1_gnn_Wr, L1_gnn_att, L1_gnn_W_up):
    import jax
    import jax.numpy as jnp

    def _L0_gnn_ref(x, edge_index, edge_type, edge_type_weights, wq, bq, wk, bk, wv, bv, wiq, biq, wik, bik, wiv, biv, wo, bo):
        import jax, jax.numpy as jnp
        import numpy as np
        N = 384
        E = 12288
        IN_F = 1024
        OUT_F = 1024
        H = 16
        D = OUT_F // H
        NUM_ETYPES = 4

        def _build_mask(edge_index, edge_type, edge_type_weights, dtype):
            src, dst = (edge_index[0], edge_index[1])
            w = jax.nn.softplus(edge_type_weights)
            mask = jnp.full((N, N), -jnp.inf, dtype=dtype)
            mask = mask.at[src, dst].set(w[edge_type - 1])
            diag = jnp.diagonal(mask)
            idx = jnp.arange(N)
            mask = mask.at[idx, idx].set(jnp.where(jnp.isneginf(diag), w[3], diag))
            return mask
        q = x @ wq.T + bq
        k = x @ wk.T + bk
        v = x @ wv.T + bv
        q2 = (q @ wiq.T + biq).reshape(N, H, D).transpose(1, 0, 2)
        k2 = (k @ wik.T + bik).reshape(N, H, D).transpose(1, 0, 2)
        v2 = (v @ wiv.T + biv).reshape(N, H, D).transpose(1, 0, 2)
        mask = _build_mask(edge_index, edge_type, edge_type_weights, x.dtype)
        scale = 1.0 / np.sqrt(D).astype(np.float32)
        scores = jnp.einsum('hnd,hmd->hnm', q2, k2) * scale + mask[None]
        attn = jax.nn.softmax(scores, axis=-1)
        out = jnp.einsum('hnm,hmd->hnd', attn, v2)
        out = out.transpose(1, 0, 2).reshape(N, OUT_F)
        return out @ wo.T + bo

    def _L1_gnn_ref(x, edge_index, rms_w, W_down, Wl, Wr, att, W_up):
        import jax, jax.numpy as jnp
        import numpy as np
        N = 2500
        E = 40000
        IN = 1024
        HID = 256
        H = 4
        D = HID // H
        OUT = 1024
        EPS = 1e-06
        NEG_SLOPE = 0.2
        n = x.shape[0]
        ms = jnp.mean(jnp.square(x), axis=-1, keepdims=True)
        x = x * jax.lax.rsqrt(ms + EPS) * rms_w
        x = x @ W_down
        loop = jnp.arange(n, dtype=edge_index.dtype)
        src = jnp.concatenate([edge_index[0], loop])
        dst = jnp.concatenate([edge_index[1], loop])
        xl = (x @ Wl).reshape(n, H, D)
        xr = (x @ Wr).reshape(n, H, D)
        msg = xl[src] + xr[dst]
        act = jnp.where(msg > 0, msg, NEG_SLOPE * msg)
        e = jnp.einsum('ehd,hd->eh', act, att)
        m = jax.ops.segment_max(e, dst, num_segments=n)
        p = jnp.exp(e - m[dst])
        denom = jax.ops.segment_sum(p, dst, num_segments=n)
        alpha = p / (denom[dst] + 1e-16)
        out = jax.ops.segment_sum(alpha[..., None] * xl[src], dst, num_segments=n)
        out = out.reshape(n, HID)
        return out @ W_up
    edge_index = jnp.stack([src, dst])
    x = _layernorm(x + _L0_gnn_ref(x, edge_index, edge_type_5, L0_gnn_edge_type_weights, L0_gnn_wq, L0_gnn_bq, L0_gnn_wk, L0_gnn_bk, L0_gnn_wv, L0_gnn_bv, L0_gnn_wiq, L0_gnn_biq, L0_gnn_wik, L0_gnn_bik, L0_gnn_wiv, L0_gnn_biv, L0_gnn_wo, L0_gnn_bo), axis=-1)
    x = _layernorm(x + _L1_gnn_ref(x, edge_index, L1_gnn_rms_w, L1_gnn_W_down, L1_gnn_Wl, L1_gnn_Wr, L1_gnn_att, L1_gnn_W_up), axis=-1)
    return x

_drawn_inputs = setup_inputs


def setup_inputs(seed=0):
    import zlib

    import numpy as np

    out = dict(_drawn_inputs(seed))
    spreads = {'L1_gnn_rms_w': (1.0, 0.6)}
    factors = {'L0_gnn_edge_type_weights': 8.0,
     'L0_gnn_wq': 5.203,
     'L0_gnn_bq': 8.0,
     'L0_gnn_wk': 5.2,
     'L0_gnn_bk': 8.0,
     'L0_gnn_bv': 7.152,
     'L0_gnn_wiq': 5.192,
     'L0_gnn_biq': 8.0,
     'L0_gnn_wik': 5.209,
     'L0_gnn_bik': 8.0,
     'L0_gnn_biv': 4.495,
     'L0_gnn_bo': 2.858,
     'L1_gnn_W_down': 3.165,
     'L1_gnn_Wl': 3.169,
     'L1_gnn_Wr': 8.0,
     'L1_gnn_att': 8.0,
     'L1_gnn_W_up': 3.167}
    for name, (base, spread) in spreads.items():
        noise = np.random.default_rng([zlib.crc32(name.encode()), seed]).standard_normal(out[name].shape)
        drawn = base * np.exp(spread * noise) if base else spread * noise
        out[name] = jnp.asarray(drawn.astype(out[name].dtype))
    for name, factor in factors.items():
        out[name] = (out[name] * factor).astype(out[name].dtype)
    return out
```

```python
from contextlib import ExitStack

import numpy as np

import concourse.bass as bass
from concourse import mybir

F32 = mybir.dt.float32
F32R = mybir.dt.float32r
I32 = mybir.dt.int32
U32 = mybir.dt.uint32
BF16 = mybir.dt.bfloat16
ALU = mybir.AluOpType
ACT = mybir.ActivationFunctionType
AX = mybir.AxisListType

P = 128
N = 384
NT = N // P
F = 1024
FT = F // P
H0, D0 = 16, 64
SCALE0 = 1.0 / 8.0
H1, D1 = 4, 64
HID = H1 * D1
HG = HID + H1
E = 6528
ET = E // P
GT = 3
EG = ET // GT
NN = N * N
FAR = -2.0e37
SLOPE = 0.2
EPS_LN = 1e-5
EPS_RMS = 1e-6
EPS_DEN = 1e-16

V0, V2_, K0, K2_, Q0, Q2_, O0, DOWN, LR, UP, CHUNKS = 0, 8, 16, 24, 32, 40, 48, 56, 58, 59, 61
RAW = 3
RING = 4
AHEAD = 3
BQ, BK, BV, BIQ, BIK, RMSW = range(6)


def evac_number(g):
    if g < V2_:
        return g
    if g < O0:
        return g - 8
    return 40 + g - DOWN


def gnn(nc, w_stream, xT, x, cols, biv, bo, etw, att, srcP, dstP, typP, srcL, dstL, out):
    ctx = ExitStack()
    with ctx:
        def sb(name, shape, dt):
            return ctx.enter_context(nc.sbuf_tensor(name, shape, dt))

        def sem(name):
            return ctx.enter_context(nc.semaphore(name))

        psum = ctx.enter_context(nc.psum_tensor("psum", [P, 8, 512], F32))
        bank = [psum[:, i, :] for i in range(8)]

        tab_mask = nc.dram_tensor("tab_mask", [NN + P, 1], F32, kind="Internal").ap()
        tab_count = nc.dram_tensor("tab_count", [NN + P, 1], F32, kind="Internal").ap()
        tab_score = [nc.dram_tensor(f"tab_score{i}", [NN + P, H1], F32, kind="Internal").ap() for i in range(2)]

        w_raw = sb("w_raw", [P, RAW, F], F32)
        w_hi = sb("w_hi", [P, RING, F], F32R)
        w_lo = sb("w_lo", [P, RING, F], F32R)
        xn = sb("xn", [P, NT, F], F32)
        colv = sb("colv", [P, 6, FT], F32)
        ident = sb("ident", [P, P], F32)
        ident_r = sb("ident_r", [P, P], F32R)
        later_mask = sb("later_mask", [P, P], BF16)
        node_id = sb("node_id", [P, NT], F32)
        dump_row = sb("dump_row", [P, 1], F32)
        self_idx = sb("self_idx", [P, NT], I32)
        w4 = sb("w4", [P, 4], F32)
        sp = sb("sp", [P, 4, 4], F32)
        ints = sb("ints", [P, 3, ET], I32)
        srcf = sb("srcf", [P, ET], F32)
        dstf = sb("dstf", [P, ET], F32)
        typf = sb("typf", [P, ET], F32)
        key0 = sb("key0", [P, ET], F32)
        key1 = sb("key1", [P, ET], F32)
        wedge = sb("wedge", [P, ET], F32)
        wtmp = sb("wtmp", [P, ET], F32)
        same = sb("same", [P, ET], F32)
        later = sb("later", [P, ET], F32)
        keep = sb("keep", [P, ET], F32)
        gap = sb("gap", [P, 2, ET], F32)
        idx0 = sb("idx0", [P, ET], I32)
        idx1 = sb("idx1", [P, ET], I32)
        eq = sb("eq", [P, GT, P], BF16)
        eql = sb("eql", [P, GT, P], BF16)
        neg_max = sb("neg_max", [P, H0, NT], F32)
        row_sum = sb("row_sum", [P, H0, NT], F32)
        inv_sum = sb("inv_sum", [P, H0, NT], F32)
        stats = sb("stats", [P, NT, 2, 6], F32)
        mv = sb("mv", [P, NT, 2], F32)
        st1 = sb("st1", [P, NT, 8], F32)
        count = sb("count", [P, NT, N], F32)
        score_e = sb("score_e", [P, GT * (EG + 1), H1], F32)
        g_att = sb("g_att", [P, NT, 2 * H1], F32)
        m1 = sb("m1", [P, NT, 4, H1], F32)

        K = 1024
        ARENA = 138 * K
        base = nc.sbuf_base
        ctx.enter_context(nc.sbuf_tensor("arena", [P, ARENA // 4], F32))

        def at(name, offset, shape, dt):
            return nc.alloc_sbuf_tensor_at(name, shape, dt, offset=base + offset)

        xT_hi = at("xT_hi", 0, [P, FT, N], F32R)
        xT_lo = at("xT_lo", 12 * K, [P, FT, N], F32R)
        oT_hi = at("oT_hi", 0, [P, FT, N], F32R)
        oT_lo = at("oT_lo", 12 * K, [P, FT, N], F32R)
        a_hi = at("a_hi", 24 * K, [P, FT, N], F32R)
        a_lo = at("a_lo", 36 * K, [P, FT, N], F32R)
        k2_hi = at("k2_hi", 48 * K, [P, FT, N], F32R)
        k2_lo = at("k2_lo", 60 * K, [P, FT, N], F32R)
        v2_hi = at("v2_hi", 72 * K, [P, NT, F], F32R)
        v2_lo = at("v2_lo", 84 * K, [P, NT, F], F32R)
        q2_hi = at("q2_hi", 96 * K, [P, 2, N], F32R)
        q2_lo = at("q2_lo", 99 * K, [P, 2, N], F32R)
        s_buf = at("s_buf", 102 * K, [P, 2, NT, N], F32)
        pt_hi = at("pt_hi", 111 * K, [P, 2, NT, N], F32R)
        pt_lo = at("pt_lo", 120 * K, [P, 2, NT, N], F32R)
        mask = at("mask", 129 * K, [P, NT, N], F32)
        bias_row = at("bias_row", 134 * K, [P, F], F32)
        xT_raw = at("xT_raw", 102 * K, [P, FT, N], F32)
        diag = at("diag", 114 * K, [P, NT, N], F32)
        init_mask = at("init_mask", 119 * K, [P, NT, N], F32)
        far = at("far", 48 * K, [P, NN * H1 // P], F32)
        onehot = at("onehot", 0, [P, 2, 2 * NT, GT * P], F32R)
        h_hi = at("h_hi", 18 * K, [P, 2, N], F32R)
        h_lo = at("h_lo", 21 * K, [P, 2, N], F32R)
        o2_hi = at("o2_hi", 0, [P, 2, N], F32R)
        o2_lo = at("o2_lo", 3 * K, [P, 2, N], F32R)
        b_hi = at("b_hi", 24 * K, [P, FT, N], F32R)
        b_lo = at("b_lo", 36 * K, [P, FT, N], F32R)
        src_row = at("src_row", 48 * K, [P, E], I32)
        dst_row = at("dst_row", 48 * K + 4 * E, [P, E], I32)
        lr_hi = at("lr_hi", 102 * K, [P, NT, 2, HG], F32R)
        lr_lo = at("lr_lo", 109 * K, [P, NT, 2, HG], F32R)
        xs = at("xs", 116 * K, [P, NT, F], F32)
        z_buf = at("z_buf", 116 * K, [P, 2, GT, HID], F32)
        za_buf = at("za_buf", 122 * K, [P, 2, GT, HID], F32)
        att_row = at("att_row", 134 * K, [P, HID], F32)
        sc0 = at("sc0", 24 * K, [P, NT, N * H1], F32)
        sc1 = at("sc1", 42 * K, [P, NT, N * H1], F32)
        p1 = at("p1", 60 * K, [P, NT, H1, N], F32)
        at_hi = at("at_hi", 78 * K, [P, 2, NT, N], F32R)
        at_lo = at("at_lo", 87 * K, [P, 2, NT, N], F32R)

        x_loaded = sem("x_loaded")
        xn_loaded = sem("xn_loaded")
        small_loaded = sem("small_loaded")
        biv_loaded = sem("biv_loaded")
        bo_loaded = sem("bo_loaded")
        att_loaded = sem("att_loaded")
        w_loaded = [sem(f"w_loaded{i}") for i in range(RAW)]
        w_hi_ready = sem("w_hi_ready")
        w_lo_ready = sem("w_lo_ready")
        xhi_ready = sem("xhi_ready")
        xlo_ready = sem("xlo_ready")
        evac_hi = sem("evac_hi")
        evac_lo = sem("evac_lo")
        proj_done = sem("proj_done")
        v2_done = sem("v2_done")
        v2_sum = sem("v2_sum")
        v2_hi_ready = sem("v2_hi_ready")
        v2_lo_ready = sem("v2_lo_ready")
        consts = sem("consts")
        pool_step = sem("pool_step")
        keys_ready = sem("keys_ready")
        softplus_in = sem("softplus_in")
        act_step = sem("act_step")
        softplus_log = sem("softplus_log")
        wsp_ready = sem("wsp_ready")
        keyrow_ready = sem("keyrow_ready")
        idx_ready = sem("idx_ready")
        init_ready = sem("init_ready")
        tab_filled = sem("tab_filled")
        mask_put = sem("mask_put")
        count_put = sem("count_put")
        mask_loaded = sem("mask_loaded")
        count_loaded = sem("count_loaded")
        xb_ready = sem("xb_ready")
        dve_step = sem("dve_step")
        qk_done = sem("qk_done")
        s_ready = sem("s_ready")
        exp_done = sem("exp_done")
        p_ready = sem("p_ready")
        t_done = sem("t_done")
        pt_hi_ready = sem("pt_hi_ready")
        pt_lo_ready = sem("pt_lo_ready")
        av_done = sem("av_done")
        oT_hi_ready = sem("oT_hi_ready")
        oT_lo_ready = sem("oT_lo_ready")
        out0_done = sem("out0_done")
        out0_part = sem("out0_part")
        y_ready = sem("y_ready")
        var_ready = sem("var_ready")
        std_ready = sem("std_ready")
        x1_ready = sem("x1_ready")
        ms_ready = sem("ms_ready")
        ms_in = sem("ms_in")
        rms_ready = sem("rms_ready")
        xs_ready = sem("xs_ready")
        bt_done = sem("bt_done")
        b_hi_ready = sem("b_hi_ready")
        b_lo_ready = sem("b_lo_ready")
        lr_done = sem("lr_done")
        g_ready = sem("g_ready")
        lr_hi_ready = sem("lr_hi_ready")
        lr_lo_ready = sem("lr_lo_ready")
        rows_loaded = sem("rows_loaded")
        onehot_ready = sem("onehot_ready")
        msg_done = sem("msg_done")
        z_ready = sem("z_ready")
        z_used = sem("z_used")
        score_ready = sem("score_ready")
        score_put = [sem(f"score_put{i}") for i in range(2)]
        scores_loaded = sem("scores_loaded")
        max1_ready = sem("max1_ready")
        exp1_done = sem("exp1_done")
        p1_ready = sem("p1_ready")
        t1_done = sem("t1_done")
        at_hi_ready = sem("at_hi_ready")
        at_lo_ready = sem("at_lo_ready")
        av1_done = sem("av1_done")
        o2_hi_ready = sem("o2_hi_ready")
        o2_lo_ready = sem("o2_lo_ready")
        up_done = sem("up_done")
        y2_ready = sem("y2_ready")
        x2_ready = sem("x2_ready")
        stored = sem("stored")

        block = ctx.enter_context(nc.Block())

        def rows(h):
            return slice(64 * (h % 2), 64 * (h % 2) + 64)

        def xT_raw_sum(i):
            return xT_raw[:].rearrange("p k n -> p (k n)")[:, 512 * i:512 * i + 512]

        def wait_used(eng, g):
            if V2_ <= g < K0:
                eng.wait_ge(v2_done, g - V2_ + 1)
            elif O0 <= g < DOWN - 1:
                eng.wait_ge(out0_part, g - O0 + 1)
            elif g == DOWN - 1:
                eng.wait_ge(out0_done, NT)
            elif g == LR:
                eng.wait_ge(lr_done, NT)
            else:
                eng.wait_ge(proj_done, evac_number(g) + 1)

        @block.sync
        def _(eng):
            def load_chunk(g):
                if g >= RAW:
                    eng.wait_ge(w_hi_ready, g - RAW + 1)
                    eng.wait_ge(w_lo_ready, g - RAW + 1)
                eng.dma_start(w_raw[:, g % RAW, :], w_stream[g]).then_inc(w_loaded[g % RAW], 16)

            eng.dma_start(xT_raw[:], xT).then_inc(x_loaded, 16)
            load_chunk(0)
            load_chunk(1)
            for g in range(2, CHUNKS):
                if g == V2_ + 1:
                    eng.dma_start(bias_row[:], biv.partition_broadcast(P)).then_inc(biv_loaded, 16)
                if g == K0 + 4:
                    eng.wait_ge(v2_sum, 6)
                    eng.dma_start(bias_row[:], bo.partition_broadcast(P)).then_inc(bo_loaded, 16)
                load_chunk(g)
                if g == DOWN + 1:
                    eng.wait_ge(av_done, H0)
                    eng.dma_start(src_row[:], srcL.partition_broadcast(P)).then_inc(rows_loaded, 16)
                    eng.dma_start(dst_row[:], dstL.partition_broadcast(P)).then_inc(rows_loaded, 16)
                    eng.wait_ge(xb_ready, 1)
                    eng.dma_start(att_row[:], att.partition_broadcast(P)).then_inc(att_loaded, 16)
            for i in range(2):
                eng.wait_ge(score_put[i], 16 * ((ET + NT + 1 - i) // 2))
            eng.wait_ge(msg_done, GT * (EG + 1))
            for sc, tab in zip((sc0, sc1), tab_score):
                for r in range(NT):
                    eng.dma_start(sc[:, r, :], tab[r * P * N:(r + 1) * P * N, :].rearrange("(p s) h -> p (s h)", p=P)) \
                       .then_inc(scores_loaded, 16)
            for r in range(NT):
                eng.wait_ge(x2_ready, r + 1)
                eng.dma_start(out[r * P:(r + 1) * P, :], xn[:, r, :]).then_inc(stored, 16)
            eng.wait_ge(stored, 16 * NT)

        @block.gpsimd
        def _(eng):
            eng.dma_start(ints[:, 0, :], srcP).then_inc(small_loaded, 16)
            eng.dma_start(ints[:, 1, :], dstP).then_inc(small_loaded, 16)
            eng.dma_start(ints[:, 2, :], typP).then_inc(small_loaded, 16)
            eng.dma_start(w4[:], etw.partition_broadcast(P)).then_inc(small_loaded, 16)
            eng.dma_start(colv[:], cols).then_inc(small_loaded, 16)
            eng.dma_start(xn[:], x.rearrange("(r p) f -> p r f", p=P)).then_inc(xn_loaded, 16)
            eng.memset(ident[:], 0.0).then_inc(pool_step, 1)
            eng.memset(later_mask[:], 0.0).then_inc(pool_step, 1)
            eng.memset(diag[:], 0.0).then_inc(pool_step, 1)
            eng.iota(node_id[:], pattern=[[P, NT]], base=0, channel_multiplier=1,
                     allow_small_or_imprecise_dtypes=True)
            eng.iota(dump_row[:], pattern=[[0, 1]], base=NN, channel_multiplier=1,
                     allow_small_or_imprecise_dtypes=True)
            for r in range(NT):
                eng.iota(self_idx[:, r:r + 1], pattern=[[0, 1]], base=r * P * (N + 1), channel_multiplier=N + 1)
            eng.wait_ge(pool_step, 3)
            eng.affine_select(out=ident[:], in_=ident[:], compare_op=ALU.not_equal, fill=1.0,
                              base=0, pattern=[[-1, P]], channel_multiplier=1).then_inc(consts, 1)
            eng.affine_select(out=later_mask[:], in_=later_mask[:], compare_op=ALU.is_ge, fill=1.0,
                              base=0, pattern=[[-1, P]], channel_multiplier=1).then_inc(consts, 1)
            eng.affine_select(out=diag[:], in_=diag[:], compare_op=ALU.not_equal, fill=1.0,
                              base=0, pattern=[[P, NT], [-1, N]], channel_multiplier=1).then_inc(consts, 1)
            eng.wait_ge(init_ready, 1)
            eng.wait_ge(consts, 3)
            eng.dma_start(tab_mask[0:NN, :].rearrange("(r p m) o -> p r (m o)", p=P, m=N), init_mask[:]) \
               .then_inc(tab_filled, 16)
            eng.dma_start(tab_count[0:NN, :].rearrange("(r p m) o -> p r (m o)", p=P, m=N), diag[:]) \
               .then_inc(tab_filled, 16)
            eng.dma_start(tab_count[NN:NN + P, :], diag[:, 0, 0:1]).then_inc(tab_filled, 16)
            for i in range(2):
                eng.dma_start(tab_score[i][0:NN, :].rearrange("(p m) h -> p (m h)", p=P), far[:]) \
                   .then_inc(tab_filled, 16)
            eng.wait_ge(tab_filled, 80)
            for t in range(ET):
                if t % GT == 0:
                    eng.wait_ge(idx_ready, t // GT + 1)
                if t >= 1:
                    eng.wait_ge(mask_put, 16 * t)
                eng.indirect_dma_start(tab_mask, bass.IndirectOffsetOnAxis(ap=idx0[:, t:t + 1].bitcast(U32), axis=0),
                                       wedge[:, t:t + 1], None).then_inc(mask_put, 16)
                if t >= 1:
                    eng.wait_ge(count_put, 16 * t)
                eng.indirect_dma_start(tab_count, bass.IndirectOffsetOnAxis(ap=idx1[:, t:t + 1].bitcast(U32), axis=0),
                                       same[:, t:t + 1], None, compute_op=ALU.add).then_inc(count_put, 16)
            eng.wait_ge(mask_put, 16 * ET)
            eng.dma_start(mask[:], tab_mask[0:NN, :].rearrange("(r p m) o -> p r (m o)", p=P, m=N)) \
               .then_inc(mask_loaded, 16)
            eng.wait_ge(count_put, 16 * ET)
            eng.dma_start(count[:], tab_count[0:NN, :].rearrange("(r p m) o -> p r (m o)", p=P, m=N)) \
               .then_inc(count_loaded, 16)
            eng.wait_ge(xn_loaded, 16)
            eng.wait_ge(bo_loaded, 16)
            for r in range(NT):
                ins = eng.tensor_tensor(xn[:, r, :], xn[:, r, :], bias_row[:], ALU.add)
            ins.then_inc(xb_ready, 1)
            for t in range(NT + ET):
                if t % GT == 0:
                    eng.wait_ge(score_ready, t // GT + 1)
                if t >= 2:
                    eng.wait_ge(score_put[t % 2], 16 * (t // 2))
                ix = self_idx[:, t:t + 1] if t < NT else idx1[:, t - NT:t - NT + 1]
                eng.indirect_dma_start(tab_score[t % 2], bass.IndirectOffsetOnAxis(ap=ix.bitcast(U32), axis=0),
                                       score_e[:, t, :], None).then_inc(score_put[t % 2], 16)

        @block.scalar
        def _(eng):
            def split(g):
                if g >= CHUNKS:
                    return
                eng.wait_ge(w_loaded[g % RAW], 16 * (g // RAW + 1))
                if g >= RING:
                    wait_used(eng, g - RING)
                eng.activation(w_hi[:, g % RING, :], w_raw[:, g % RAW, :], ACT.Copy).then_inc(w_hi_ready, 1)

            def evac(g, dst, bias):
                n = evac_number(g)
                eng.wait_ge(proj_done, n + 1)
                eng.activation(dst, bank[n % 2][:, 0:N], ACT.Identity, bias=bias).then_inc(evac_hi, 1)

            eng.wait_ge(x_loaded, 16)
            for c in range(2):
                eng.activation(xT_hi[:, 4 * c:4 * c + 4, :], xT_raw[:, 4 * c:4 * c + 4, :], ACT.Copy).then_inc(xhi_ready, 1)
                split(c)
            for g in range(2, AHEAD):
                split(g)
            eng.wait_ge(softplus_in, 1)
            eng.activation(sp[:, 1, :], sp[:, 0, :], ACT.Exp, scale=-1.0).then_inc(act_step, 1)
            eng.wait_ge(act_step, 1)
            eng.activation(sp[:, 2, :], sp[:, 1, :], ACT.Ln, bias=1.0).then_inc(softplus_log, 1)
            eng.wait_ge(small_loaded, 80)
            for g in range(V0, V2_):
                split(g + AHEAD)
                evac(g, a_hi[:, g - V0, :], colv[:, BV, g - V0:g - V0 + 1])
            for g in range(V2_, K0):
                split(g + AHEAD)
            for i in range(6):
                eng.wait_ge(v2_sum, i + 1)
                r, c = divmod(i, 2)
                eng.activation(v2_hi[:, r, 512 * c:512 * c + 512], xT_raw_sum(i), ACT.Copy).then_inc(v2_hi_ready, 1)
            for g in range(K0, K2_):
                split(g + AHEAD)
                evac(g, a_hi[:, g - K0, :], colv[:, BK, g - K0:g - K0 + 1])
            eng.wait_ge(tab_filled, 80)
            for g in range(K2_, Q0):
                split(g + AHEAD)
                evac(g, k2_hi[:, g - K2_, :], colv[:, BIK, g - K2_:g - K2_ + 1])
            for g in range(Q0, Q2_):
                split(g + AHEAD)
                evac(g, a_hi[:, g - Q0, :], colv[:, BQ, g - Q0:g - Q0 + 1])
            split(Q2_ + AHEAD)
            evac(Q2_, q2_hi[:, 0, :], colv[:, BIQ, 0:1])
            for h in range(H0 + 2):
                if h < H0:
                    for r in range(NT):
                        eng.wait_ge(s_ready, NT * h + r + 1)
                        eng.activation(s_buf[:, h % 2, r, :], s_buf[:, h % 2, r, :], ACT.Exp, scale=-1.0,
                                       bias=neg_max[:, h, r:r + 1], accum_out=row_sum[:, h, r:r + 1]).then_inc(exp_done, 1)
                    if h % 2 == 1 and h < H0 - 1:
                        t = h // 2 + 1
                        evac(Q2_ + t, q2_hi[:, t % 2, :], colv[:, BIQ, t:t + 1])
                if 1 <= h <= H0:
                    for i in range(NT):
                        c = NT * (h - 1) + i
                        eng.wait_ge(t_done, c + 1)
                        if h >= 3:
                            eng.wait_ge(av_done, h - 2)
                        eng.activation(pt_hi[:, (h - 1) % 2, i, :], bank[5 + c % 2][:, 0:N], ACT.Copy).then_inc(pt_hi_ready, 1)
                if h >= 2:
                    eng.wait_ge(av_done, h - 1)
                    eng.activation(oT_hi[rows(h - 2), (h - 2) // 2, :], bank[7][rows(h - 2), 0:N], ACT.Copy) \
                       .then_inc(oT_hi_ready, 1)
                if h % 2 == 1 and h < H0 - 1:
                    split(Q2_ + h // 2 + 1 + AHEAD)
            for g in range(O0, DOWN):
                split(g + AHEAD)
            for r in range(NT):
                eng.wait_ge(var_ready, r + 1)
                eng.activation(st1[:, r, 1:2], st1[:, r, 0:1], ACT.Sqrt).then_inc(std_ready, 1)
            for r in range(NT):
                eng.wait_ge(x1_ready, r + 1)
                eng.activation(xs[:, r, :], xn[:, r, :], ACT.Square, accum_out=st1[:, r, 3:4]).then_inc(ms_ready, 1)
                eng.wait_ge(ms_in, r + 1)
                eng.activation(st1[:, r, 5:6], st1[:, r, 4:5], ACT.Sqrt).then_inc(rms_ready, 1)
            for ft in range(FT):
                eng.wait_ge(bt_done, ft + 1)
                eng.activation(b_hi[:, ft, :], bank[ft][:, 0:N], ACT.Copy, scale=colv[:, RMSW, ft:ft + 1]).then_inc(b_hi_ready, 1)
            for g in range(DOWN, LR):
                split(g + AHEAD)
                n = evac_number(g)
                eng.wait_ge(proj_done, n + 1)
                eng.activation(h_hi[:, g - DOWN, :], bank[n % 2][:, 0:N], ACT.Copy).then_inc(evac_hi, 1)
            for r in range(NT):
                eng.wait_ge(lr_done, r + 1)
                eng.activation(lr_hi[:, r, :, 0:HID], bank[2 + r].rearrange("p (s f) -> p s f", s=2), ACT.Copy) \
                   .then_inc(lr_hi_ready, 1)
                eng.wait_ge(g_ready, r + 1)
                eng.activation(lr_hi[:, r, :, HID:HG], g_att[:, r, :].rearrange("p (s h) -> p s h", s=2), ACT.Copy) \
                   .then_inc(lr_hi_ready, 1)
            for g in range(EG + 1):
                for i in range(GT):
                    eng.wait_ge(msg_done, GT * g + i + 1)
                    if g >= 2:
                        eng.wait_ge(z_used, g - 1)
                    eng.activation(z_buf[:, g % 2, i, :], bank[GT * (g % 2) + i][:, 0:HID], ACT.Relu, scale=1.0 - SLOPE) \
                       .then_inc(z_ready, 1)
            for r in range(NT):
                eng.wait_ge(max1_ready, r + 1)
                for h in range(H1):
                    eng.activation(p1[:, r, h, :], sc0[:, r, :].rearrange("p (s h) -> p h s", h=H1)[:, h, :], ACT.Exp,
                                   bias=m1[:, r, 1, h:h + 1]).then_inc(exp1_done, 1)
            for h in range(H1 + 1):
                if h < H1:
                    for i in range(NT):
                        c = NT * h + i
                        eng.wait_ge(t1_done, c + 1)
                        if h >= 2:
                            eng.wait_ge(av1_done, h - 1)
                        eng.activation(at_hi[:, h % 2, i, :], bank[c % 4][:, 0:N], ACT.Copy).then_inc(at_hi_ready, 1)
                if h >= 1:
                    k = h - 1
                    eng.wait_ge(av1_done, k + 1)
                    eng.activation(o2_hi[rows(k), k // 2, :], bank[6 + k % 2][rows(k), 0:N], ACT.Copy).then_inc(o2_hi_ready, 1)
            for r in range(NT):
                eng.wait_ge(var_ready, NT + r + 1)
                eng.activation(st1[:, r, 1:2], st1[:, r, 0:1], ACT.Sqrt).then_inc(std_ready, 1)

        @block.vector
        def _(eng):
            steps = [0]

            def link(ins):
                steps[0] += 1
                ins.then_inc(dve_step, 1)
                eng.wait_ge(dve_step, steps[0])

            def split(g):
                if g >= CHUNKS:
                    return
                eng.wait_ge(w_hi_ready, g + 1)
                eng.tensor_tensor(w_lo[:, g % RING, :], w_raw[:, g % RAW, :], w_hi[:, g % RING, :].bitcast(F32),
                                  ALU.subtract).then_inc(w_lo_ready, 1)

            def evac(g, dst, hi, bias):
                n = evac_number(g)
                eng.wait_ge(evac_hi, n + 1)
                eng.scalar_tensor_tensor(out=dst, in0=bank[n % 2][:, 0:N], scalar=bias, in1=hi.bitcast(F32),
                                         op0=ALU.add, op1=ALU.subtract).then_inc(evac_lo, 1)

            def dedupe(j):
                if j >= EG:
                    return
                s = slice(GT * j, GT * j + GT)
                b = bank[6 + j % 2][:, 0:GT * P].rearrange("p (t e) -> p t e", t=GT)
                eng.wait_ge(keyrow_ready, j + 1)
                link(eng.tensor_tensor(eq[:], b, key0[:, s].unsqueeze(2).to_broadcast([P, GT, P]), ALU.is_equal))
                link(eng.tensor_tensor(eql[:], eq[:], later_mask[:].unsqueeze(1).to_broadcast([P, GT, P]), ALU.mult))
                eng.tensor_reduce(same[:, s], eq[:], AX.X, ALU.add)
                link(eng.tensor_reduce(later[:, s], eql[:], AX.X, ALU.add))
                link(eng.tensor_scalar(keep[:, s], later[:, s], 0.0, None, ALU.is_equal))
                eng.tensor_tensor(gap[:, 0, s], gap[:, 0, s], keep[:, s], ALU.mult)
                link(eng.tensor_tensor(gap[:, 1, s], gap[:, 1, s], keep[:, s], ALU.mult))
                eng.tensor_scalar(idx0[:, s], gap[:, 0, s], dump_row[:, 0:1], None, ALU.add)
                eng.tensor_scalar(idx1[:, s], gap[:, 1, s], dump_row[:, 0:1], None, ALU.add).then_inc(idx_ready, 1)

            eng.memset(far[:], FAR).then_inc(dve_step, 1)
            steps[0] += 1
            eng.wait_ge(small_loaded, 80)
            eng.tensor_copy(srcf[:], ints[:, 0, :])
            eng.tensor_copy(dstf[:], ints[:, 1, :])
            link(eng.tensor_copy(typf[:], ints[:, 2, :]))
            eng.scalar_tensor_tensor(out=key0[:], in0=srcf[:], scalar=float(N), in1=dstf[:], op0=ALU.mult,
                                     op1=ALU.add).then_inc(keys_ready, 1)
            link(eng.scalar_tensor_tensor(out=key1[:], in0=dstf[:], scalar=float(N), in1=srcf[:], op0=ALU.mult,
                                          op1=ALU.add))
            eng.scalar_tensor_tensor(out=sp[:, 0, :], in0=w4[:], scalar=-1.0, in1=w4[:], op0=ALU.mult,
                                     op1=ALU.max).then_inc(softplus_in, 1)
            for c in range(2):
                eng.wait_ge(xhi_ready, c + 1)
                eng.tensor_tensor(xT_lo[:, 4 * c:4 * c + 4, :], xT_raw[:, 4 * c:4 * c + 4, :],
                                  xT_hi[:, 4 * c:4 * c + 4, :].bitcast(F32), ALU.subtract).then_inc(xlo_ready, 1)
                split(c)
            for g in range(2, AHEAD):
                split(g)
            eng.wait_ge(consts, 3)
            eng.wait_ge(softplus_log, 1)
            link(eng.scalar_tensor_tensor(out=sp[:, 3, :], in0=w4[:], scalar=0.0, in1=sp[:, 2, :], op0=ALU.max,
                                          op1=ALU.add))
            link(eng.tensor_scalar(sp[:, 2, :], sp[:, 3, :], 1.0 / SCALE0, None, ALU.mult))
            link(eng.tensor_scalar(init_mask[:], diag[:], -FAR, FAR, ALU.mult, ALU.add))
            eng.scalar_tensor_tensor(out=init_mask[:], in0=diag[:], scalar=sp[:, 2, 3:4], in1=init_mask[:],
                                     op0=ALU.mult, op1=ALU.add).then_inc(init_ready, 1)
            eng.tensor_scalar(gap[:, 0, :], key0[:], dump_row[:, 0:1], None, ALU.subtract)
            eng.tensor_scalar(gap[:, 1, :], key1[:], dump_row[:, 0:1], None, ALU.subtract)
            link(eng.tensor_scalar(wedge[:], typf[:], 0.0, sp[:, 2, 3:4], ALU.is_equal, ALU.mult))
            for k in range(1, 5):
                link(eng.tensor_scalar(wtmp[:], typf[:], float(k), sp[:, 2, k - 1:k], ALU.is_equal, ALU.mult))
                link(eng.tensor_tensor(wedge[:], wedge[:], wtmp[:], ALU.add))

            for g in range(V0, V2_):
                split(g + AHEAD)
                dedupe(g - V0)
                evac(g, a_lo[:, g - V0, :], a_hi[:, g - V0, :], colv[:, BV, g - V0:g - V0 + 1])
            for g in range(V2_, K0):
                split(g + AHEAD)
                dedupe(g - V0)
            eng.wait_ge(v2_done, FT)
            eng.wait_ge(biv_loaded, 16)
            for i in range(6):
                r, c = divmod(i, 2)
                eng.tensor_tensor(xT_raw_sum(i), bank[i], bias_row[:, 512 * c:512 * c + 512], ALU.add) \
                   .then_inc(v2_sum, 1)
            for i in range(6):
                r, c = divmod(i, 2)
                eng.wait_ge(v2_hi_ready, i + 1)
                eng.tensor_tensor(v2_lo[:, r, 512 * c:512 * c + 512], xT_raw_sum(i),
                                  v2_hi[:, r, 512 * c:512 * c + 512].bitcast(F32), ALU.subtract).then_inc(v2_lo_ready, 1)
            dedupe(EG - 1)
            for g in range(K0, K2_):
                split(g + AHEAD)
                evac(g, a_lo[:, g - K0, :], a_hi[:, g - K0, :], colv[:, BK, g - K0:g - K0 + 1])
            eng.wait_ge(tab_filled, 80)
            for g in range(K2_, Q0):
                split(g + AHEAD)
                evac(g, k2_lo[:, g - K2_, :], k2_hi[:, g - K2_, :], colv[:, BIK, g - K2_:g - K2_ + 1])
            for g in range(Q0, Q2_):
                split(g + AHEAD)
                evac(g, a_lo[:, g - Q0, :], a_hi[:, g - Q0, :], colv[:, BQ, g - Q0:g - Q0 + 1])
            split(Q2_ + AHEAD)
            evac(Q2_, q2_lo[:, 0, :], q2_hi[:, 0, :], colv[:, BIQ, 0:1])
            eng.wait_ge(mask_loaded, 16)
            for h in range(H0 + 2):
                if 1 <= h <= H0:
                    k = h - 1
                    eng.wait_ge(exp_done, NT * (k + 1))
                    link(eng.reciprocal(inv_sum[:, k, :], row_sum[:, k, :]))
                    for r in range(NT):
                        ins = eng.tensor_scalar(s_buf[:, k % 2, r, :], s_buf[:, k % 2, r, :], inv_sum[:, k, r:r + 1],
                                                None, ALU.mult)
                    ins.then_inc(p_ready, 1)
                if h < H0:
                    for r in range(NT):
                        eng.wait_ge(qk_done, NT * h + r + 1)
                        if h >= 2:
                            eng.wait_ge(t_done, NT * (h - 1))
                        eng.tensor_tensor_reduce(s_buf[:, h % 2, r, :], bank[2 + r][:, 0:N], mask[:, r, :], -SCALE0,
                                                 -FAR, ALU.add, ALU.min, neg_max[:, h, r:r + 1]).then_inc(s_ready, 1)
                    if h % 2 == 1 and h < H0 - 1:
                        t = h // 2 + 1
                        evac(Q2_ + t, q2_lo[:, t % 2, :], q2_hi[:, t % 2, :], colv[:, BIQ, t:t + 1])
                if 1 <= h <= H0:
                    for i in range(NT):
                        c = NT * (h - 1) + i
                        eng.wait_ge(pt_hi_ready, c + 1)
                        eng.tensor_tensor(pt_lo[:, (h - 1) % 2, i, :], bank[5 + c % 2][:, 0:N],
                                          pt_hi[:, (h - 1) % 2, i, :].bitcast(F32), ALU.subtract).then_inc(pt_lo_ready, 1)
                if h >= 2:
                    k = h - 2
                    eng.wait_ge(oT_hi_ready, k + 1)
                    eng.tensor_tensor(oT_lo[rows(k), k // 2, :], bank[7][rows(k), 0:N],
                                      oT_hi[rows(k), k // 2, :].bitcast(F32), ALU.subtract).then_inc(oT_lo_ready, 1)
                if h % 2 == 1 and h < H0 - 1:
                    split(Q2_ + h // 2 + 1 + AHEAD)
            for g in range(O0, DOWN):
                split(g + AHEAD)

            def layernorm_stats(r):
                for c in range(2):
                    ins = eng.bn_stats(stats[:, r, c, :], xn[:, r, 512 * c:512 * c + 512])
                link(ins)
                link(eng.bn_aggr(mv[:, r, :], stats[:, r, :, :]))
                eng.tensor_scalar(st1[:, r, 0:1], mv[:, r, 1:2], EPS_LN, None, ALU.add).then_inc(var_ready, 1)

            def layernorm_apply(r, n, done):
                eng.wait_ge(std_ready, n)
                link(eng.reciprocal(st1[:, r, 2:3], st1[:, r, 1:2]))
                eng.tensor_scalar(xn[:, r, :], xn[:, r, :], mv[:, r, 0:1], st1[:, r, 2:3], ALU.subtract,
                                  ALU.mult).then_inc(done, 1)

            eng.wait_ge(xb_ready, 1)
            for r in range(NT):
                eng.wait_ge(out0_done, r + 1)
                for c in range(2):
                    ins = eng.tensor_tensor(xn[:, r, 512 * c:512 * c + 512], bank[2 * r + c],
                                            xn[:, r, 512 * c:512 * c + 512], ALU.add)
                link(ins)
                layernorm_stats(r)
            for r in range(NT):
                layernorm_apply(r, r + 1, x1_ready)
            for r in range(NT):
                eng.wait_ge(ms_ready, r + 1)
                eng.tensor_scalar(st1[:, r, 4:5], st1[:, r, 3:4], 1.0 / F, EPS_RMS, ALU.mult, ALU.add).then_inc(ms_in, 1)
            for r in range(NT):
                eng.wait_ge(rms_ready, r + 1)
                link(eng.reciprocal(st1[:, r, 6:7], st1[:, r, 5:6]))
                eng.tensor_scalar(xs[:, r, :], xn[:, r, :], st1[:, r, 6:7], None, ALU.mult).then_inc(xs_ready, 1)

            def onehots(g):
                if g >= EG:
                    return
                if g >= 2:
                    eng.wait_ge(msg_done, GT * g)
                for s, row in enumerate((src_row, dst_row)):
                    for r in range(NT):
                        ins = eng.tensor_scalar(onehot[:, g % 2, NT * s + r, :], row[:, GT * P * g:GT * P * (g + 1)],
                                                node_id[:, r:r + 1], None, ALU.is_equal)
                ins.then_inc(onehot_ready, 1)

            for ft in range(FT):
                eng.wait_ge(b_hi_ready, ft + 1)
                eng.scalar_tensor_tensor(out=b_lo[:, ft, :], in0=bank[ft][:, 0:N], scalar=colv[:, RMSW, ft:ft + 1],
                                         in1=b_hi[:, ft, :].bitcast(F32), op0=ALU.mult, op1=ALU.subtract) \
                   .then_inc(b_lo_ready, 1)
            eng.tensor_copy(ident_r[:], ident[:]).then_inc(dve_step, 1)
            steps[0] += 1
            ident_step = steps[0]
            eng.wait_ge(rows_loaded, 32)
            onehots(0)
            onehots(1)
            for g in range(DOWN, LR):
                split(g + AHEAD)
                n = evac_number(g)
                eng.wait_ge(evac_hi, n + 1)
                eng.tensor_tensor(h_lo[:, g - DOWN, :], bank[n % 2][:, 0:N], h_hi[:, g - DOWN, :].bitcast(F32),
                                  ALU.subtract).then_inc(evac_lo, 1)
            eng.wait_ge(att_loaded, 16)
            for r in range(NT):
                eng.wait_ge(lr_hi_ready, 2 * r + 1)
                link(eng.tensor_tensor(za_buf[:, 0, 0:2, :], bank[2 + r].rearrange("p (s f) -> p s f", s=2),
                                       att_row[:].unsqueeze(1).to_broadcast([P, 2, HID]), ALU.mult))
                eng.tensor_reduce(g_att[:, r, :], za_buf[:, 0, 0:2, :].rearrange("p s (h d) -> p (s h) d", h=H1),
                                  AX.X, ALU.add).then_inc(g_ready, 1)
                eng.wait_ge(lr_hi_ready, 2 * r + 2)
                eng.tensor_tensor(lr_lo[:, r, :, 0:HID], bank[2 + r].rearrange("p (s f) -> p s f", s=2),
                                  lr_hi[:, r, :, 0:HID].bitcast(F32), ALU.subtract)
                eng.tensor_tensor(lr_lo[:, r, :, HID:HG], g_att[:, r, :].rearrange("p (s h) -> p s h", s=2),
                                  lr_hi[:, r, :, HID:HG].bitcast(F32), ALU.subtract).then_inc(lr_lo_ready, 1)
            for g in range(EG + 1):
                if g >= 1:
                    onehots(g + 1)
                eng.wait_ge(z_ready, GT * (g + 1))
                ins = eng.tensor_tensor(za_buf[:, g % 2, :, :], z_buf[:, g % 2, :, :],
                                        att_row[:].unsqueeze(1).to_broadcast([P, GT, HID]), ALU.mult)
                ins.then_inc(z_used, 1)
                eng.wait_ge(z_used, g + 1)
                link(eng.tensor_reduce(score_e[:, GT * g:GT * g + GT, :],
                                       za_buf[:, g % 2, :, :].rearrange("p t (h d) -> p t h d", h=H1), AX.X, ALU.add))
                eng.scalar_tensor_tensor(out=score_e[:, GT * g:GT * g + GT, :],
                                         in0=psum[:, GT * (g % 2):GT * (g % 2) + GT, HID:HG], scalar=SLOPE,
                                         in1=score_e[:, GT * g:GT * g + GT, :], op0=ALU.mult, op1=ALU.add) \
                   .then_inc(score_ready, 1)
            eng.wait_ge(scores_loaded, 16 * 2 * NT)
            eng.wait_ge(count_loaded, 16)
            for r in range(NT):
                link(eng.tensor_tensor(sc0[:, r, :], sc0[:, r, :], sc1[:, r, :], ALU.max))
                link(eng.tensor_reduce(m1[:, r, 0, :], sc0[:, r, :].rearrange("p (s h) -> p h s", h=H1), AX.X, ALU.max))
                eng.tensor_scalar(m1[:, r, 1, :], m1[:, r, 0, :], -1.0, None, ALU.mult).then_inc(max1_ready, 1)
            for r in range(NT):
                for h in range(H1):
                    eng.wait_ge(exp1_done, H1 * r + h + 1)
                    ins = eng.tensor_tensor_reduce(p1[:, r, h, :], p1[:, r, h, :], count[:, r, :], 1.0, 0.0,
                                                   ALU.mult, ALU.add, m1[:, r, 2, h:h + 1])
                link(ins)
                link(eng.tensor_scalar(m1[:, r, 2, :], m1[:, r, 2, :], EPS_DEN, None, ALU.add))
                link(eng.reciprocal(m1[:, r, 3, :], m1[:, r, 2, :]))
                for h in range(H1):
                    eng.tensor_scalar(p1[:, r, h, :], p1[:, r, h, :], m1[:, r, 3, h:h + 1], None, ALU.mult) \
                       .then_inc(p1_ready, 1)
            for h in range(H1 + 1):
                if h < H1:
                    for i in range(NT):
                        c = NT * h + i
                        eng.wait_ge(at_hi_ready, c + 1)
                        eng.tensor_tensor(at_lo[:, h % 2, i, :], bank[c % 4][:, 0:N], at_hi[:, h % 2, i, :].bitcast(F32),
                                          ALU.subtract).then_inc(at_lo_ready, 1)
                if h >= 1:
                    k = h - 1
                    eng.wait_ge(o2_hi_ready, k + 1)
                    eng.tensor_tensor(o2_lo[rows(k), k // 2, :], bank[6 + k % 2][rows(k), 0:N],
                                      o2_hi[rows(k), k // 2, :].bitcast(F32), ALU.subtract).then_inc(o2_lo_ready, 1)
            for r in range(NT):
                eng.wait_ge(up_done, r + 1)
                for c in range(2):
                    ins = eng.tensor_tensor(xn[:, r, 512 * c:512 * c + 512], bank[2 * r + c],
                                            xn[:, r, 512 * c:512 * c + 512], ALU.add)
                link(ins)
                layernorm_stats(r)
            for r in range(NT):
                layernorm_apply(r, NT + r + 1, x2_ready)

        @block.tensor
        def _(eng):
            def product(dst, a, b, start, stop):
                eng.matmul(dst, a[0], b[0], start=start, stop=False)
                eng.matmul(dst, a[0], b[1], start=False, stop=False)
                return eng.matmul(dst, a[1], b[0], start=False, stop=stop)

            def chunk(g, f):
                return w_hi[:, g % RING, f], w_lo[:, g % RING, f]

            def wait_chunk(g):
                eng.wait_ge(w_hi_ready, g + 1)
                eng.wait_ge(w_lo_ready, g + 1)

            def free_bank(g):
                n = evac_number(g)
                if n >= 2:
                    eng.wait_ge(evac_lo, n - 1)

            def project(g, src, kts, inputs_evac=None):
                b = bank[evac_number(g) % 2][:, 0:N]
                for kt in kts:
                    if inputs_evac is not None:
                        eng.wait_ge(evac_lo, inputs_evac + kt + 1)
                    mm = product(b, chunk(g, slice(kt * P, kt * P + P)), (src[0][:, kt, :], src[1][:, kt, :]),
                                 kt == 0, kt == FT - 1)
                if kts[-1] == FT - 1:
                    mm.then_inc(proj_done, 1)

            def keyrows(j):
                if j >= EG:
                    return
                if j >= 2:
                    eng.wait_ge(idx_ready, j - 1)
                for i in range(GT):
                    t = GT * j + i
                    mm = eng.matmul(bank[6 + j % 2][:, P * i:P * i + P], key0[:, t:t + 1].to_broadcast([P, P]), ident[:],
                                    start=True, stop=True)
                mm.then_inc(keyrow_ready, 1)

            every = list(range(FT))
            eng.wait_ge(keys_ready, 1)
            eng.wait_ge(consts, 1)
            keyrows(0)
            keyrows(1)
            for g in range(V0, V2_):
                if g == V0:
                    eng.wait_ge(xlo_ready, 2)
                wait_chunk(g)
                free_bank(g)
                project(g, (xT_hi, xT_lo), every)
                keyrows(g - V0 + 2)
            eng.wait_ge(evac_lo, FT)
            for g in range(V2_, K0):
                kt = g - V2_
                wait_chunk(g)
                for r in range(NT):
                    a = (a_hi[:, kt, r * P:r * P + P], a_lo[:, kt, r * P:r * P + P])
                    for c in range(2):
                        mm = product(bank[2 * r + c], a, chunk(g, slice(512 * c, 512 * c + 512)), kt == 0, kt == FT - 1)
                mm.then_inc(v2_done, 1)
                keyrows(g - V0 + 2)
            eng.wait_ge(v2_sum, 6)
            for g in range(K0, K2_):
                wait_chunk(g)
                free_bank(g)
                project(g, (xT_hi, xT_lo), every)
            for g in range(K2_, Q0):
                wait_chunk(g)
                free_bank(g)
                project(g, (a_hi, a_lo), every, evac_number(K0) if g == K2_ else None)
            for g in range(Q0, Q2_):
                wait_chunk(g)
                free_bank(g)
                project(g, (xT_hi, xT_lo), every)
            wait_chunk(Q2_)
            free_bank(Q2_)
            project(Q2_, (a_hi, a_lo), every, evac_number(Q0))
            eng.wait_ge(v2_lo_ready, 6)
            eng.wait_ge(idx_ready, EG)
            for h in range(H0 + 2):
                t = h // 2
                if h < H0:
                    eng.wait_ge(evac_lo, evac_number(Q2_) + t + 1)
                    for r in range(NT):
                        if h >= 1:
                            eng.wait_ge(s_ready, NT * (h - 1) + r + 1)
                        q = (q2_hi[rows(h), t % 2, r * P:r * P + P], q2_lo[rows(h), t % 2, r * P:r * P + P])
                        product(bank[2 + r][:, 0:N], q, (k2_hi[rows(h), t, :], k2_lo[rows(h), t, :]), True, True) \
                            .then_inc(qk_done, 1)
                    if t + 1 < FT:
                        g = Q2_ + t + 1
                        if h % 2 == 0:
                            wait_chunk(g)
                            free_bank(g)
                        project(g, (a_hi, a_lo), every[4 * (h % 2):4 * (h % 2) + 4])
                if 1 <= h <= H0:
                    k = h - 1
                    eng.wait_ge(p_ready, k + 1)
                    for i in range(NT):
                        c = NT * k + i
                        if c >= 2:
                            eng.wait_ge(pt_lo_ready, c - 1)
                        for r in range(NT):
                            mm = eng.transpose(bank[5 + c % 2][:, r * P:r * P + P], s_buf[:, k % 2, r, i * P:i * P + P], ident[:])
                        mm.then_inc(t_done, 1)
                if h >= 2:
                    k = h - 2
                    if k >= 1:
                        eng.wait_ge(oT_lo_ready, k)
                    c = slice(k // 2 * P, k // 2 * P + P)
                    for i in range(NT):
                        eng.wait_ge(pt_lo_ready, NT * k + i + 1)
                        mm = product(bank[7][:, 0:N], (v2_hi[:, i, c], v2_lo[:, i, c]),
                                     (pt_hi[:, k % 2, i, :], pt_lo[:, k % 2, i, :]), i == 0, i == NT - 1)
                    mm.then_inc(av_done, 1)
            for g in range(O0, DOWN):
                kt = g - O0
                wait_chunk(g)
                eng.wait_ge(oT_lo_ready, 2 * kt + 2)
                for r in range(NT):
                    a = (oT_hi[:, kt, r * P:r * P + P], oT_lo[:, kt, r * P:r * P + P])
                    for c in range(2):
                        mm = product(bank[2 * r + c], a, chunk(g, slice(512 * c, 512 * c + 512)), kt == 0, kt == FT - 1)
                    if kt == FT - 1:
                        mm.then_inc(out0_done, 1)
                if kt < FT - 1:
                    mm.then_inc(out0_part, 1)
            for r in range(NT):
                eng.wait_ge(xs_ready, r + 1)
                for ft in range(FT):
                    mm = eng.transpose(bank[ft][:, r * P:r * P + P], xs[:, r, ft * P:ft * P + P], ident[:])
                    if r == NT - 1:
                        mm.then_inc(bt_done, 1)
            for g in range(DOWN, LR):
                wait_chunk(g)
                b = bank[evac_number(g) % 2][:, 0:N]
                for kt in range(FT):
                    eng.wait_ge(b_lo_ready, kt + 1)
                    mm = product(b, chunk(g, slice(kt * P, kt * P + P)), (b_hi[:, kt, :], b_lo[:, kt, :]), kt == 0, kt == FT - 1)
                mm.then_inc(proj_done, 1)
            wait_chunk(LR)
            eng.wait_ge(b_lo_ready, FT)
            for r in range(NT):
                for f in range(2):
                    eng.wait_ge(evac_lo, evac_number(DOWN) + f + 1)
                    mm = product(bank[2 + r], (h_hi[:, f, r * P:r * P + P], h_lo[:, f, r * P:r * P + P]),
                                 chunk(LR, slice(512 * f, 512 * f + 512)), f == 0, f == 1)
                mm.then_inc(lr_done, 1)
            for g in range(EG + 1):
                if g >= 1:
                    eng.wait_ge(onehot_ready, g)
                for i in range(GT):
                    if g == 0:
                        eng.wait_ge(lr_lo_ready, i + 1)
                    if g >= 2:
                        eng.wait_ge(score_ready, g - 1)
                    b = bank[GT * (g % 2) + i][:, 0:HG]
                    if g == 0:
                        parts = [(ident_r[:], s, i) for s in range(2)]
                        eng.wait_ge(lr_lo_ready, NT)
                    else:
                        parts = [(onehot[:, (g - 1) % 2, NT * s + r, i * P:i * P + P], s, r)
                                 for s in range(2) for r in range(NT)]
                    for n, (hot, s, r) in enumerate(parts):
                        eng.matmul(b, hot, lr_hi[:, r, s, :], start=(n == 0), stop=False)
                        mm = eng.matmul(b, hot, lr_lo[:, r, s, :], start=False, stop=(n == len(parts) - 1))
                    mm.then_inc(msg_done, 1)
            for h in range(H1 + 1):
                if h < H1:
                    eng.wait_ge(p1_ready, H1 * (NT - 1) + h + 1)
                    for i in range(NT):
                        c = NT * h + i
                        if c >= 4:
                            eng.wait_ge(at_lo_ready, c - 3)
                        for r in range(NT):
                            mm = eng.transpose(bank[c % 4][:, r * P:r * P + P], p1[:, r, h, i * P:i * P + P], ident[:])
                        mm.then_inc(t1_done, 1)
                if h >= 1:
                    k = h - 1
                    if k >= 2:
                        eng.wait_ge(o2_lo_ready, k - 1)
                    c = slice(k // 2 * P, k // 2 * P + P)
                    for i in range(NT):
                        eng.wait_ge(at_lo_ready, NT * k + i + 1)
                        mm = product(bank[6 + k % 2][:, 0:N], (lr_hi[:, i, 0, c], lr_lo[:, i, 0, c]),
                                     (at_hi[:, k % 2, i, :], at_lo[:, k % 2, i, :]), i == 0, i == NT - 1)
                    mm.then_inc(av1_done, 1)
            wait_chunk(UP + 1)
            eng.wait_ge(o2_lo_ready, H1)
            for r in range(NT):
                for c in range(2):
                    for f in range(2):
                        mm = product(bank[2 * r + c], (o2_hi[:, f, r * P:r * P + P], o2_lo[:, f, r * P:r * P + P]),
                                     chunk(UP + f, slice(512 * c, 512 * c + 512)), f == 0, f == 1)
                mm.then_inc(up_done, 1)


def kernel(**inputs):
    import concourse.bacc as bacc
    from concourse.bass_utils import run_bass_kernel_spmd

    a = {k: np.asarray(v) for k, v in inputs.items()}

    def by_out_tile(wT):
        i, o = wT.shape
        return wT.reshape(i // P, P, o // P, P).transpose(2, 1, 0, 3).reshape(o // P, P, -1)

    def by_in_tile(wT):
        return wT.reshape(wT.shape[0] // P, P, -1)

    g0 = {k[7:]: v for k, v in a.items() if k.startswith("L0_gnn_")}
    g1 = {k[7:]: v for k, v in a.items() if k.startswith("L1_gnn_")}
    lr = np.concatenate([g1["Wl"], g1["Wr"]], axis=1)
    w_stream = np.concatenate([
        by_out_tile(g0["wv"].T), by_in_tile(g0["wiv"].T), by_out_tile(g0["wk"].T), by_out_tile(g0["wik"].T),
        by_out_tile(g0["wq"].T), by_out_tile(g0["wiq"].T), by_in_tile(g0["wo"].T), by_out_tile(g1["W_down"]),
        lr.reshape(2, P, 2 * HID).transpose(1, 0, 2).reshape(1, P, -1), by_in_tile(g1["W_up"]),
    ])
    vectors = [g0["bq"], g0["bk"], g0["bv"], g0["biq"], g0["bik"], g1["rms_w"]]
    arrays = {
        "w_stream": w_stream,
        "xT": a["x"].T.reshape(FT, P, N).transpose(1, 0, 2),
        "x": a["x"],
        "cols": np.stack([v.reshape(FT, P).T for v in vectors], axis=1),
        "biv": g0["biv"], "bo": g0["bo"], "etw": g0["edge_type_weights"], "att": g1["att"].reshape(-1),
        "srcP": a["src"][:E].reshape(ET, P).T, "dstP": a["dst"][:E].reshape(ET, P).T,
        "typP": a["edge_type_5"].reshape(ET, P).T, "srcL": a["src"], "dstL": a["dst"],
    }
    arrays = {k: np.ascontiguousarray(v) for k, v in arrays.items()}
    nc = bacc.Bacc("TRN2", target_bir_lowering=False, num_devices=1)
    args = [nc.dram_tensor(f"in_{k}", v.shape, mybir.dt.from_np(v.dtype), kind="ExternalInput").ap()
            for k, v in arrays.items()]
    out = nc.dram_tensor("out_x", (N, F), F32, kind="ExternalOutput").ap()
    gnn(nc, *args, out)
    got = run_bass_kernel_spmd(nc, [{f"in_{k}": v for k, v in arrays.items()}], core_ids=[0])
    return got.results[0]["out_x"]
```

```python
from contextlib import ExitStack

import numpy as np

import concourse.bass as bass
from concourse import mybir

F32 = mybir.dt.float32
F32R = mybir.dt.float32r
I32 = mybir.dt.int32
U32 = mybir.dt.uint32
BF16 = mybir.dt.bfloat16
ALU = mybir.AluOpType
ACT = mybir.ActivationFunctionType
AX = mybir.AxisListType

P = 128
N = 384
NT = N // P
F = 1024
FT = F // P
H0, D0 = 16, 64
SCALE0 = 1.0 / 8.0
H1, D1 = 4, 64
HID = H1 * D1
HG = HID + H1
E = 6528
ET = E // P
GT = 3
EG = ET // GT
NN = N * N
FAR = -2.0e37
SLOPE = 0.2
EPS_LN = 1e-5
EPS_RMS = 1e-6
EPS_DEN = 1e-16

V0, V2_, K0, K2_, Q0, Q2_, O0, DOWN, LR, UP, CHUNKS = 0, 8, 16, 24, 32, 40, 48, 56, 58, 59, 61
RAW = 3
RING = 4
AHEAD = 3
FT_ORDER = [6, 7, 0, 1, 2, 3, 4, 5]
BQ, BK, BV, BIQ, BIK, RMSW = range(6)


def evac_number(g):
    if g < V2_:
        return g
    if g < O0:
        return g - 8
    return 40 + g - DOWN


def gnn(nc, w_stream, xT, x, cols, biv, bo, etw, att, srcP, dstP, typP, srcL, dstL, out):
    ctx = ExitStack()
    with ctx:
        def sb(name, shape, dt):
            return ctx.enter_context(nc.sbuf_tensor(name, shape, dt))

        def sem(name):
            return ctx.enter_context(nc.semaphore(name))

        psum = ctx.enter_context(nc.psum_tensor("psum", [P, 8, 512], F32))
        bank = [psum[:, i, :] for i in range(8)]

        tab_mask = nc.dram_tensor("tab_mask", [NN + P, 1], F32, kind="Internal").ap()
        tab_count = nc.dram_tensor("tab_count", [NN + P, 1], F32, kind="Internal").ap()
        tab_score = [nc.dram_tensor(f"tab_score{i}", [NN + P, H1], F32, kind="Internal").ap() for i in range(2)]

        w_raw = sb("w_raw", [P, RAW, F], F32)
        w_hi = sb("w_hi", [P, RING, F], F32R)
        w_lo = sb("w_lo", [P, RING, F], F32R)
        xn = sb("xn", [P, NT, F], F32)
        colv = sb("colv", [P, 6, FT], F32)
        ident = sb("ident", [P, P], F32)
        ident_r = sb("ident_r", [P, P], F32R)
        later_mask = sb("later_mask", [P, P], BF16)
        node_id = sb("node_id", [P, NT], F32)
        dump_row = sb("dump_row", [P, 1], F32)
        self_idx = sb("self_idx", [P, NT], I32)
        w4 = sb("w4", [P, 4], F32)
        sp = sb("sp", [P, 4, 4], F32)
        ints = sb("ints", [P, 3, ET], I32)
        srcf = sb("srcf", [P, ET], F32)
        dstf = sb("dstf", [P, ET], F32)
        typf = sb("typf", [P, ET], F32)
        key0 = sb("key0", [P, ET], F32)
        key1 = sb("key1", [P, ET], F32)
        wedge = sb("wedge", [P, ET], F32)
        wtmp = sb("wtmp", [P, ET], F32)
        same = sb("same", [P, ET], F32)
        later = sb("later", [P, ET], F32)
        keep = sb("keep", [P, ET], F32)
        gap = sb("gap", [P, 2, ET], F32)
        idx0 = sb("idx0", [P, ET], I32)
        idx1 = sb("idx1", [P, ET], I32)
        eq = sb("eq", [P, GT, P], BF16)
        eql = sb("eql", [P, GT, P], BF16)
        neg_max = sb("neg_max", [P, H0, NT], F32)
        row_sum = sb("row_sum", [P, H0, NT], F32)
        inv_sum = sb("inv_sum", [P, H0, NT], F32)
        stats = sb("stats", [P, NT, 2, 6], F32)
        mv = sb("mv", [P, NT, 2], F32)
        st1 = sb("st1", [P, NT, 8], F32)
        count = sb("count", [P, NT, N], F32)
        score_e = sb("score_e", [P, GT * (EG + 1), H1], F32)
        g_att = sb("g_att", [P, NT, 2 * H1], F32)
        m1 = sb("m1", [P, NT, 4, H1], F32)

        K = 1024
        ARENA = 138 * K
        base = nc.sbuf_base
        ctx.enter_context(nc.sbuf_tensor("arena", [P, ARENA // 4], F32))

        def at(name, offset, shape, dt):
            return nc.alloc_sbuf_tensor_at(name, shape, dt, offset=base + offset)

        xT_hi = at("xT_hi", 0, [P, FT, N], F32R)
        xT_lo = at("xT_lo", 12 * K, [P, FT, N], F32R)
        oT_hi = at("oT_hi", 0, [P, FT, N], F32R)
        oT_lo = at("oT_lo", 12 * K, [P, FT, N], F32R)
        a_hi = at("a_hi", 24 * K, [P, FT, N], F32R)
        a_lo = at("a_lo", 36 * K, [P, FT, N], F32R)
        k2_hi = at("k2_hi", 48 * K, [P, FT, N], F32R)
        k2_lo = at("k2_lo", 60 * K, [P, FT, N], F32R)
        v2_hi = at("v2_hi", 72 * K, [P, NT, F], F32R)
        v2_lo = at("v2_lo", 84 * K, [P, NT, F], F32R)
        q2_hi = at("q2_hi", 96 * K, [P, 2, N], F32R)
        q2_lo = at("q2_lo", 99 * K, [P, 2, N], F32R)
        s_buf = at("s_buf", 102 * K, [P, 2, NT, N], F32)
        pt_hi = at("pt_hi", 111 * K, [P, 2, NT, N], F32R)
        pt_lo = at("pt_lo", 120 * K, [P, 2, NT, N], F32R)
        mask = at("mask", 129 * K, [P, NT, N], F32)
        bias_row = at("bias_row", 134 * K, [P, F], F32)
        xT_raw = at("xT_raw", 102 * K, [P, FT, N], F32)
        diag = at("diag", 114 * K, [P, NT, N], F32)
        init_mask = at("init_mask", 119 * K, [P, NT, N], F32)
        far = at("far", 48 * K, [P, NN * H1 // P], F32)
        onehot = at("onehot", 0, [P, 2, 2 * NT, GT * P], F32R)
        h_hi = at("h_hi", 18 * K, [P, 2, N], F32R)
        h_lo = at("h_lo", 21 * K, [P, 2, N], F32R)
        o2_hi = at("o2_hi", 0, [P, 2, N], F32R)
        o2_lo = at("o2_lo", 3 * K, [P, 2, N], F32R)
        b_hi = at("b_hi", 24 * K, [P, FT, N], F32R)
        b_lo = at("b_lo", 36 * K, [P, FT, N], F32R)
        src_row = at("src_row", 48 * K, [P, E], I32)
        dst_row = at("dst_row", 48 * K + 4 * E, [P, E], I32)
        lr_hi = at("lr_hi", 102 * K, [P, NT, 2, HG], F32R)
        lr_lo = at("lr_lo", 109 * K, [P, NT, 2, HG], F32R)
        xs = at("xs", 116 * K, [P, NT, F], F32)
        z_buf = at("z_buf", 116 * K, [P, 2, GT, HID], F32)
        za_buf = at("za_buf", 122 * K, [P, 2, GT, HID], F32)
        att_row = at("att_row", 134 * K, [P, HID], F32)
        sc0 = at("sc0", 24 * K, [P, NT, N * H1], F32)
        sc1 = at("sc1", 42 * K, [P, NT, N * H1], F32)
        p1 = at("p1", 60 * K, [P, NT, H1, N], F32)
        at_hi = at("at_hi", 78 * K, [P, 2, NT, N], F32R)
        at_lo = at("at_lo", 87 * K, [P, 2, NT, N], F32R)

        x_loaded = [sem(f"x_loaded{i}") for i in range(2)]
        xn_loaded = sem("xn_loaded")
        small_loaded = sem("small_loaded")
        biv_loaded = sem("biv_loaded")
        bo_loaded = sem("bo_loaded")
        att_loaded = sem("att_loaded")
        w_loaded = [sem(f"w_loaded{i}") for i in range(RAW)]
        w_hi_ready = sem("w_hi_ready")
        w_lo_ready = sem("w_lo_ready")
        xhi_ready = sem("xhi_ready")
        xlo_ready = sem("xlo_ready")
        evac_hi = sem("evac_hi")
        evac_lo = sem("evac_lo")
        proj_done = sem("proj_done")
        v2_done = sem("v2_done")
        v2_sum = sem("v2_sum")
        v2_hi_ready = sem("v2_hi_ready")
        v2_lo_ready = sem("v2_lo_ready")
        consts = sem("consts")
        ident_ready = sem("ident_ready")
        pool_step = sem("pool_step")
        keys_ready = sem("keys_ready")
        softplus_in = sem("softplus_in")
        act_step = sem("act_step")
        softplus_log = sem("softplus_log")
        wsp_ready = sem("wsp_ready")
        keyrow_ready = sem("keyrow_ready")
        idx_ready = sem("idx_ready")
        init_ready = sem("init_ready")
        tab_filled = sem("tab_filled")
        mask_put = sem("mask_put")
        count_put = sem("count_put")
        mask_loaded = sem("mask_loaded")
        count_loaded = sem("count_loaded")
        xb_ready = sem("xb_ready")
        dve_step = sem("dve_step")
        qk_done = sem("qk_done")
        s_ready = sem("s_ready")
        exp_done = sem("exp_done")
        p_ready = sem("p_ready")
        t_done = sem("t_done")
        pt_hi_ready = sem("pt_hi_ready")
        pt_lo_ready = sem("pt_lo_ready")
        av_done = sem("av_done")
        oT_hi_ready = sem("oT_hi_ready")
        oT_lo_ready = sem("oT_lo_ready")
        out0_done = sem("out0_done")
        out0_part = sem("out0_part")
        var_ready = sem("var_ready")
        std_ready = sem("std_ready")
        xs_ready = sem("xs_ready")
        bt_done = sem("bt_done")
        b_hi_ready = sem("b_hi_ready")
        b_lo_ready = sem("b_lo_ready")
        lr_done = sem("lr_done")
        g_ready = sem("g_ready")
        lr_hi_ready = sem("lr_hi_ready")
        lr_lo_ready = sem("lr_lo_ready")
        rows_loaded = sem("rows_loaded")
        onehot_ready = sem("onehot_ready")
        msg_done = sem("msg_done")
        z_ready = sem("z_ready")
        z_used = sem("z_used")
        score_ready = sem("score_ready")
        score_put = [sem(f"score_put{i}") for i in range(2)]
        scores_loaded = [sem(f"scores_loaded{r}") for r in range(NT)]
        max1_ready = sem("max1_ready")
        exp1_done = sem("exp1_done")
        sum1_ready = sem("sum1_ready")
        p1_ready = sem("p1_ready")
        t1_done = sem("t1_done")
        at_hi_ready = sem("at_hi_ready")
        at_lo_ready = sem("at_lo_ready")
        av1_done = sem("av1_done")
        o2_hi_ready = sem("o2_hi_ready")
        o2_lo_ready = sem("o2_lo_ready")
        up_done = sem("up_done")
        x2_ready = sem("x2_ready")
        stored = sem("stored")

        block = ctx.enter_context(nc.Block())

        def tile_ahead(h):
            return 1 if h == 0 else h // 2 + 1 if h % 2 == 1 and 1 < h < H0 - 1 else None

        def rows(h):
            return slice(64 * (h % 2), 64 * (h % 2) + 64)

        def xT_raw_sum(i):
            return xT_raw[:].rearrange("p k n -> p (k n)")[:, 512 * i:512 * i + 512]

        def wait_used(eng, g):
            if V2_ <= g < K0:
                eng.wait_ge(v2_done, g - V2_ + 1)
            elif O0 <= g < O0 + RING:
                eng.wait_ge(out0_part, g - O0 + 1)
            elif O0 + RING <= g < DOWN:
                eng.wait_ge(out0_done, 2 * NT)
            elif g == LR:
                eng.wait_ge(lr_done, NT)
            else:
                eng.wait_ge(proj_done, evac_number(g) + 1)

        @block.sync
        def _(eng):
            def load_chunk(g):
                if g >= RAW:
                    eng.wait_ge(w_hi_ready, g - RAW + 1)
                    eng.wait_ge(w_lo_ready, g - RAW + 1)
                eng.dma_start(w_raw[:, g % RAW, :], w_stream[g]).then_inc(w_loaded[g % RAW], 16)

            for c in range(2):
                eng.dma_start(xT_raw[:, 4 * c:4 * c + 4, :], xT[:, 4 * c:4 * c + 4, :]).then_inc(x_loaded[c], 16)
                if c == 0:
                    load_chunk(0)
            load_chunk(1)
            for g in range(2, CHUNKS):
                if g == V2_ + 1:
                    eng.dma_start(bias_row[:], biv.partition_broadcast(P)).then_inc(biv_loaded, 16)
                if g == K0 + 4:
                    eng.wait_ge(v2_sum, 6)
                    eng.dma_start(bias_row[:], bo.partition_broadcast(P)).then_inc(bo_loaded, 16)
                load_chunk(g)
                if g == DOWN + 1:
                    eng.wait_ge(av_done, H0)
                    eng.dma_start(src_row[:], srcL.partition_broadcast(P)).then_inc(rows_loaded, 16)
                    eng.dma_start(dst_row[:], dstL.partition_broadcast(P)).then_inc(rows_loaded, 16)
                    eng.wait_ge(xb_ready, 1)
                    eng.dma_start(att_row[:], att.partition_broadcast(P)).then_inc(att_loaded, 16)
            for i in range(2):
                eng.wait_ge(score_put[i], 16 * ((ET + NT + 1 - i) // 2))
            eng.wait_ge(msg_done, GT * (EG + 1))
            for r in range(NT):
                for sc, tab in zip((sc0, sc1), tab_score):
                    eng.dma_start(sc[:, r, :], tab[r * P * N:(r + 1) * P * N, :].rearrange("(p s) h -> p (s h)", p=P)) \
                       .then_inc(scores_loaded[r], 16)
            for r in range(NT):
                eng.wait_ge(x2_ready, r + 1)
                eng.dma_start(out[r * P:(r + 1) * P, :], xn[:, r, :]).then_inc(stored, 16)
            eng.wait_ge(stored, 16 * NT)

        @block.gpsimd
        def _(eng):
            eng.dma_start(ints[:, 0, :], srcP).then_inc(small_loaded, 16)
            eng.dma_start(ints[:, 1, :], dstP).then_inc(small_loaded, 16)
            eng.dma_start(ints[:, 2, :], typP).then_inc(small_loaded, 16)
            eng.dma_start(w4[:], etw.partition_broadcast(P)).then_inc(small_loaded, 16)
            eng.dma_start(colv[:], cols).then_inc(small_loaded, 16)
            eng.dma_start(xn[:], x.rearrange("(r p) f -> p r f", p=P)).then_inc(xn_loaded, 16)
            eng.memset(ident[:], 0.0).then_inc(pool_step, 1)
            eng.memset(later_mask[:], 0.0).then_inc(pool_step, 1)
            eng.memset(diag[:], 0.0).then_inc(pool_step, 1)
            eng.iota(node_id[:], pattern=[[P, NT]], base=0, channel_multiplier=1,
                     allow_small_or_imprecise_dtypes=True)
            eng.iota(dump_row[:], pattern=[[0, 1]], base=NN, channel_multiplier=1,
                     allow_small_or_imprecise_dtypes=True)
            for r in range(NT):
                eng.iota(self_idx[:, r:r + 1], pattern=[[0, 1]], base=r * P * (N + 1), channel_multiplier=N + 1)
            eng.wait_ge(pool_step, 3)
            eng.affine_select(out=ident[:], in_=ident[:], compare_op=ALU.not_equal, fill=1.0,
                              base=0, pattern=[[-1, P]], channel_multiplier=1).then_inc(consts, 1)
            eng.affine_select(out=later_mask[:], in_=later_mask[:], compare_op=ALU.is_ge, fill=1.0,
                              base=0, pattern=[[-1, P]], channel_multiplier=1).then_inc(consts, 1)
            eng.affine_select(out=diag[:], in_=diag[:], compare_op=ALU.not_equal, fill=1.0,
                              base=0, pattern=[[P, NT], [-1, N]], channel_multiplier=1).then_inc(consts, 1)
            eng.memset(far[:], FAR).then_inc(pool_step, 1)
            eng.wait_ge(pool_step, 4)
            eng.wait_ge(init_ready, 1)
            eng.wait_ge(consts, 3)
            eng.dma_start(tab_mask[0:NN, :].rearrange("(r p m) o -> p r (m o)", p=P, m=N), init_mask[:]) \
               .then_inc(tab_filled, 16)
            eng.dma_start(tab_count[0:NN, :].rearrange("(r p m) o -> p r (m o)", p=P, m=N), diag[:]) \
               .then_inc(tab_filled, 16)
            eng.dma_start(tab_count[NN:NN + P, :], diag[:, 0, 0:1]).then_inc(tab_filled, 16)
            for i in range(2):
                eng.dma_start(tab_score[i][0:NN, :].rearrange("(p m) h -> p (m h)", p=P), far[:]) \
                   .then_inc(tab_filled, 16)
            eng.wait_ge(tab_filled, 80)
            for t in range(ET):
                if t % GT == 0:
                    eng.wait_ge(idx_ready, t // GT + 1)
                if t >= 1:
                    eng.wait_ge(mask_put, 16 * t)
                eng.indirect_dma_start(tab_mask, bass.IndirectOffsetOnAxis(ap=idx0[:, t:t + 1].bitcast(U32), axis=0),
                                       wedge[:, t:t + 1], None).then_inc(mask_put, 16)
                if t >= 1:
                    eng.wait_ge(count_put, 16 * t)
                eng.indirect_dma_start(tab_count, bass.IndirectOffsetOnAxis(ap=idx1[:, t:t + 1].bitcast(U32), axis=0),
                                       same[:, t:t + 1], None, compute_op=ALU.add).then_inc(count_put, 16)
            eng.wait_ge(mask_put, 16 * ET)
            eng.dma_start(mask[:], tab_mask[0:NN, :].rearrange("(r p m) o -> p r (m o)", p=P, m=N)) \
               .then_inc(mask_loaded, 16)
            eng.wait_ge(count_put, 16 * ET)
            eng.dma_start(count[:], tab_count[0:NN, :].rearrange("(r p m) o -> p r (m o)", p=P, m=N)) \
               .then_inc(count_loaded, 16)
            eng.wait_ge(xn_loaded, 16)
            eng.wait_ge(bo_loaded, 16)
            for r in range(NT):
                ins = eng.tensor_tensor(xn[:, r, :], xn[:, r, :], bias_row[:], ALU.add)
            ins.then_inc(xb_ready, 1)
            for t in range(NT + ET):
                if t % GT == 0:
                    eng.wait_ge(score_ready, t // GT + 1)
                if t >= 2:
                    eng.wait_ge(score_put[t % 2], 16 * (t // 2))
                ix = self_idx[:, t:t + 1] if t < NT else idx1[:, t - NT:t - NT + 1]
                eng.indirect_dma_start(tab_score[t % 2], bass.IndirectOffsetOnAxis(ap=ix.bitcast(U32), axis=0),
                                       score_e[:, t, :], None).then_inc(score_put[t % 2], 16)

        @block.scalar
        def _(eng):
            def split(g):
                if g >= CHUNKS:
                    return
                eng.wait_ge(w_loaded[g % RAW], 16 * (g // RAW + 1))
                if g >= RING:
                    wait_used(eng, g - RING)
                eng.activation(w_hi[:, g % RING, :], w_raw[:, g % RAW, :], ACT.Copy).then_inc(w_hi_ready, 1)

            def evac(g, dst, bias):
                n = evac_number(g)
                eng.wait_ge(proj_done, n + 1)
                eng.activation(dst, bank[n % 2][:, 0:N], ACT.Identity, bias=bias).then_inc(evac_hi, 1)

            for c in range(2):
                eng.wait_ge(x_loaded[c], 16)
                eng.activation(xT_hi[:, 4 * c:4 * c + 4, :], xT_raw[:, 4 * c:4 * c + 4, :], ACT.Copy).then_inc(xhi_ready, 1)
                split(c)
            for g in range(2, AHEAD):
                split(g)
            eng.wait_ge(softplus_in, 1)
            eng.activation(sp[:, 1, :], sp[:, 0, :], ACT.Exp, scale=-1.0).then_inc(act_step, 1)
            eng.wait_ge(act_step, 1)
            eng.activation(sp[:, 2, :], sp[:, 1, :], ACT.Ln, bias=1.0).then_inc(softplus_log, 1)
            eng.wait_ge(small_loaded, 80)
            for g in range(V0, V2_):
                split(g + AHEAD)
                evac(g, a_hi[:, g - V0, :], colv[:, BV, g - V0:g - V0 + 1])
            for g in range(V2_, K0):
                split(g + AHEAD)
            for i in range(6):
                eng.wait_ge(v2_sum, i + 1)
                r, c = divmod(i, 2)
                eng.activation(v2_hi[:, r, 512 * c:512 * c + 512], xT_raw_sum(i), ACT.Copy).then_inc(v2_hi_ready, 1)
            for g in range(K0, K2_):
                split(g + AHEAD)
                evac(g, a_hi[:, g - K0, :], colv[:, BK, g - K0:g - K0 + 1])
            eng.wait_ge(tab_filled, 80)
            for g in range(K2_, Q0):
                split(g + AHEAD)
                evac(g, k2_hi[:, g - K2_, :], colv[:, BIK, g - K2_:g - K2_ + 1])
            for g in range(Q0, Q2_):
                split(g + AHEAD)
                evac(g, a_hi[:, g - Q0, :], colv[:, BQ, g - Q0:g - Q0 + 1])
            split(Q2_ + AHEAD)
            evac(Q2_, q2_hi[:, 0, :], colv[:, BIQ, 0:1])
            def out_hi(k):
                eng.wait_ge(av_done, k + 1)
                eng.activation(oT_hi[rows(k), k // 2, :], bank[7][rows(k), 0:N], ACT.Copy).then_inc(oT_hi_ready, 1)

            def prob_hi(k, i):
                c = NT * k + i
                eng.wait_ge(t_done, c + 1)
                eng.activation(pt_hi[:, k % 2, i, :], bank[5 + c % 2][:, 0:N], ACT.Copy).then_inc(pt_hi_ready, 1)

            def exponential(h, r):
                eng.wait_ge(s_ready, NT * h + r + 1)
                eng.activation(s_buf[:, h % 2, r, :], s_buf[:, h % 2, r, :], ACT.Exp, scale=-1.0,
                               bias=neg_max[:, h, r:r + 1], accum_out=row_sum[:, h, r:r + 1]).then_inc(exp_done, 1)

            for h in range(H0 + 1):
                if h >= 2:
                    out_hi(h - 2)
                if h >= 1:
                    prob_hi(h - 1, 0)
                    prob_hi(h - 1, 1)
                if h < H0:
                    exponential(h, 0)
                if h >= 1:
                    prob_hi(h - 1, 2)
                if h < H0:
                    exponential(h, 1)
                    exponential(h, 2)
                if (t := tile_ahead(h)) is not None:
                    evac(Q2_ + t, q2_hi[:, t % 2, :], colv[:, BIQ, t:t + 1])
                    split(Q2_ + t + AHEAD)
                if h == H0 - 2:
                    split(O0 + RING - 1)
            out_hi(H0 - 1)
            for g in range(O0 + RING, DOWN):
                split(g)
            for r in range(NT):
                eng.wait_ge(var_ready, r + 1)
                eng.activation(st1[:, r, 2:4], st1[:, r, 0:2], ACT.Sqrt).then_inc(std_ready, 1)
            split(DOWN)
            split(DOWN + 1)
            for n, ft in enumerate(FT_ORDER):
                eng.wait_ge(bt_done, n + 1)
                eng.activation(b_hi[:, ft, :], bank[ft][:, 0:N], ACT.Copy, scale=colv[:, RMSW, ft:ft + 1]).then_inc(b_hi_ready, 1)
            split(LR)
            split(UP)
            for f in range(2):
                eng.wait_ge(proj_done, evac_number(DOWN + f) + 1)
                eng.activation(h_hi[:, f, :], bank[6 + f][:, 0:N], ACT.Copy).then_inc(evac_hi, 1)
            split(UP + 1)
            for r in range(NT):
                eng.wait_ge(lr_done, r + 1)
                eng.activation(lr_hi[:, r, :, 0:HID], bank[2 + r].rearrange("p (s f) -> p s f", s=2), ACT.Copy) \
                   .then_inc(lr_hi_ready, 1)
                eng.wait_ge(g_ready, r + 1)
                eng.activation(lr_hi[:, r, :, HID:HG], g_att[:, r, :].rearrange("p (s h) -> p s h", s=2), ACT.Copy) \
                   .then_inc(lr_hi_ready, 1)
            for g in range(EG + 1):
                for i in range(GT):
                    eng.wait_ge(msg_done, GT * g + i + 1)
                    if g >= 2:
                        eng.wait_ge(z_used, g - 1)
                    eng.activation(z_buf[:, g % 2, i, :], bank[GT * (g % 2) + i][:, 0:HID], ACT.Relu, scale=1.0 - SLOPE) \
                       .then_inc(z_ready, 1)
            def exponential1(r):
                eng.wait_ge(max1_ready, r + 1)
                for h in range(H1):
                    eng.activation(p1[:, r, h, :], sc0[:, r, :].rearrange("p (s h) -> p h s", h=H1)[:, h, :], ACT.Exp,
                                   bias=m1[:, r, 1, h:h + 1]).then_inc(exp1_done, 1)

            def normalise1(r):
                eng.wait_ge(sum1_ready, r + 1)
                for h in range(H1):
                    eng.activation(p1[:, r, h, :], p1[:, r, h, :], ACT.Copy, scale=m1[:, r, 3, h:h + 1]).then_inc(p1_ready, 1)

            exponential1(0)
            exponential1(1)
            normalise1(0)
            exponential1(2)
            normalise1(1)
            normalise1(2)
            for h in range(H1 + 1):
                if h < H1:
                    for i in range(NT):
                        c = NT * h + i
                        eng.wait_ge(t1_done, c + 1)
                        if h >= 2:
                            eng.wait_ge(av1_done, h - 1)
                        eng.activation(at_hi[:, h % 2, i, :], bank[c % 4][:, 0:N], ACT.Copy).then_inc(at_hi_ready, 1)
                if h >= 1:
                    k = h - 1
                    eng.wait_ge(av1_done, k + 1)
                    eng.activation(o2_hi[rows(k), k // 2, :], bank[6 + k % 2][rows(k), 0:N], ACT.Copy).then_inc(o2_hi_ready, 1)
            for r in range(NT):
                eng.wait_ge(var_ready, NT + r + 1)
                eng.activation(st1[:, r, 2:3], st1[:, r, 0:1], ACT.Sqrt).then_inc(std_ready, 1)

        @block.vector
        def _(eng):
            steps = [0]

            def link(ins):
                steps[0] += 1
                ins.then_inc(dve_step, 1)
                eng.wait_ge(dve_step, steps[0])

            def split(g):
                if g >= CHUNKS:
                    return
                eng.wait_ge(w_hi_ready, g + 1)
                eng.tensor_tensor(w_lo[:, g % RING, :], w_raw[:, g % RAW, :], w_hi[:, g % RING, :].bitcast(F32),
                                  ALU.subtract).then_inc(w_lo_ready, 1)

            def evac(g, dst, hi, bias):
                n = evac_number(g)
                eng.wait_ge(evac_hi, n + 1)
                eng.scalar_tensor_tensor(out=dst, in0=bank[n % 2][:, 0:N], scalar=bias, in1=hi.bitcast(F32),
                                         op0=ALU.add, op1=ALU.subtract).then_inc(evac_lo, 1)

            def dedupe(j):
                if j >= EG:
                    return
                s = slice(GT * j, GT * j + GT)
                b = bank[6 + j % 2][:, 0:GT * P].rearrange("p (t e) -> p t e", t=GT)
                eng.wait_ge(keyrow_ready, j + 1)
                link(eng.tensor_tensor(eq[:], b, key0[:, s].unsqueeze(2).to_broadcast([P, GT, P]), ALU.is_equal))
                link(eng.tensor_tensor(eql[:], eq[:], later_mask[:].unsqueeze(1).to_broadcast([P, GT, P]), ALU.mult))
                eng.tensor_reduce(same[:, s], eq[:], AX.X, ALU.add)
                link(eng.tensor_reduce(later[:, s], eql[:], AX.X, ALU.add))
                link(eng.tensor_scalar(keep[:, s], later[:, s], 0.0, None, ALU.is_equal))
                eng.tensor_tensor(gap[:, 0, s], gap[:, 0, s], keep[:, s], ALU.mult)
                link(eng.tensor_tensor(gap[:, 1, s], gap[:, 1, s], keep[:, s], ALU.mult))
                eng.tensor_scalar(idx0[:, s], gap[:, 0, s], dump_row[:, 0:1], None, ALU.add)
                eng.tensor_scalar(idx1[:, s], gap[:, 1, s], dump_row[:, 0:1], None, ALU.add).then_inc(idx_ready, 1)

            for c in range(2):
                eng.wait_ge(xhi_ready, c + 1)
                eng.tensor_tensor(xT_lo[:, 4 * c:4 * c + 4, :], xT_raw[:, 4 * c:4 * c + 4, :],
                                  xT_hi[:, 4 * c:4 * c + 4, :].bitcast(F32), ALU.subtract).then_inc(xlo_ready, 1)
                if c == 0:
                    split(0)
            eng.wait_ge(small_loaded, 80)
            eng.tensor_copy(srcf[:], ints[:, 0, :])
            eng.tensor_copy(dstf[:], ints[:, 1, :])
            link(eng.tensor_copy(typf[:], ints[:, 2, :]))
            eng.scalar_tensor_tensor(out=key0[:], in0=srcf[:], scalar=float(N), in1=dstf[:], op0=ALU.mult,
                                     op1=ALU.add).then_inc(keys_ready, 1)
            link(eng.scalar_tensor_tensor(out=key1[:], in0=dstf[:], scalar=float(N), in1=srcf[:], op0=ALU.mult,
                                          op1=ALU.add))
            eng.scalar_tensor_tensor(out=sp[:, 0, :], in0=w4[:], scalar=-1.0, in1=w4[:], op0=ALU.mult,
                                     op1=ALU.max).then_inc(softplus_in, 1)
            for g in range(1, AHEAD):
                split(g)
            eng.wait_ge(consts, 3)
            eng.wait_ge(softplus_log, 1)
            link(eng.scalar_tensor_tensor(out=sp[:, 3, :], in0=w4[:], scalar=0.0, in1=sp[:, 2, :], op0=ALU.max,
                                          op1=ALU.add))
            link(eng.tensor_scalar(sp[:, 2, :], sp[:, 3, :], 1.0 / SCALE0, None, ALU.mult))
            link(eng.tensor_scalar(init_mask[:], diag[:], -FAR, FAR, ALU.mult, ALU.add))
            eng.scalar_tensor_tensor(out=init_mask[:], in0=diag[:], scalar=sp[:, 2, 3:4], in1=init_mask[:],
                                     op0=ALU.mult, op1=ALU.add).then_inc(init_ready, 1)
            eng.tensor_scalar(gap[:, 0, :], key0[:], dump_row[:, 0:1], None, ALU.subtract)
            eng.tensor_scalar(gap[:, 1, :], key1[:], dump_row[:, 0:1], None, ALU.subtract)
            link(eng.tensor_scalar(wedge[:], typf[:], 0.0, sp[:, 2, 3:4], ALU.is_equal, ALU.mult))
            for k in range(1, 5):
                link(eng.tensor_scalar(wtmp[:], typf[:], float(k), sp[:, 2, k - 1:k], ALU.is_equal, ALU.mult))
                link(eng.tensor_tensor(wedge[:], wedge[:], wtmp[:], ALU.add))

            for g in range(V0, V2_):
                split(g + AHEAD)
                if g > V0:
                    dedupe(g - V0 - 1)
                evac(g, a_lo[:, g - V0, :], a_hi[:, g - V0, :], colv[:, BV, g - V0:g - V0 + 1])
            for g in range(V2_, K0):
                split(g + AHEAD)
                dedupe(g - V0 - 1)
            eng.wait_ge(v2_done, FT)
            eng.wait_ge(biv_loaded, 16)
            for i in range(6):
                r, c = divmod(i, 2)
                eng.tensor_tensor(xT_raw_sum(i), bank[i], bias_row[:, 512 * c:512 * c + 512], ALU.add) \
                   .then_inc(v2_sum, 1)
            for i in range(6):
                r, c = divmod(i, 2)
                eng.wait_ge(v2_hi_ready, i + 1)
                eng.tensor_tensor(v2_lo[:, r, 512 * c:512 * c + 512], xT_raw_sum(i),
                                  v2_hi[:, r, 512 * c:512 * c + 512].bitcast(F32), ALU.subtract).then_inc(v2_lo_ready, 1)
            dedupe(EG - 2)
            dedupe(EG - 1)
            for g in range(K0, K2_):
                split(g + AHEAD)
                evac(g, a_lo[:, g - K0, :], a_hi[:, g - K0, :], colv[:, BK, g - K0:g - K0 + 1])
            eng.wait_ge(tab_filled, 80)
            for g in range(K2_, Q0):
                split(g + AHEAD)
                evac(g, k2_lo[:, g - K2_, :], k2_hi[:, g - K2_, :], colv[:, BIK, g - K2_:g - K2_ + 1])
            for g in range(Q0, Q2_):
                split(g + AHEAD)
                evac(g, a_lo[:, g - Q0, :], a_hi[:, g - Q0, :], colv[:, BQ, g - Q0:g - Q0 + 1])
            split(Q2_ + AHEAD)
            evac(Q2_, q2_lo[:, 0, :], q2_hi[:, 0, :], colv[:, BIQ, 0:1])
            eng.wait_ge(mask_loaded, 16)
            def out_lo(k):
                eng.wait_ge(oT_hi_ready, k + 1)
                eng.tensor_tensor(oT_lo[rows(k), k // 2, :], bank[7][rows(k), 0:N],
                                  oT_hi[rows(k), k // 2, :].bitcast(F32), ALU.subtract).then_inc(oT_lo_ready, 1)

            def prob_lo(k, i):
                c = NT * k + i
                eng.wait_ge(pt_hi_ready, c + 1)
                eng.tensor_tensor(pt_lo[:, k % 2, i, :], bank[5 + c % 2][:, 0:N], pt_hi[:, k % 2, i, :].bitcast(F32),
                                  ALU.subtract).then_inc(pt_lo_ready, 1)

            def score(h, r):
                eng.wait_ge(qk_done, NT * h + r + 1)
                eng.tensor_tensor_reduce(s_buf[:, h % 2, r, :], bank[2 + r][:, 0:N], mask[:, r, :], -SCALE0,
                                         -FAR, ALU.add, ALU.min, neg_max[:, h, r:r + 1]).then_inc(s_ready, 1)

            for h in range(H0 + 1):
                if h >= 2:
                    out_lo(h - 2)
                if h >= 1:
                    prob_lo(h - 1, 0)
                if h < H0:
                    score(h, 0)
                if h >= 1:
                    prob_lo(h - 1, 1)
                if h < H0:
                    score(h, 1)
                    score(h, 2)
                if h >= 1:
                    prob_lo(h - 1, 2)
                if (t := tile_ahead(h)) is not None:
                    evac(Q2_ + t, q2_lo[:, t % 2, :], q2_hi[:, t % 2, :], colv[:, BIQ, t:t + 1])
                    if h > 0:
                        split(Q2_ + t + AHEAD)
                if h < H0:
                    eng.wait_ge(exp_done, NT * (h + 1))
                    link(eng.reciprocal(inv_sum[:, h, :], row_sum[:, h, :]))
                    for r in range(NT):
                        ins = eng.tensor_scalar(s_buf[:, h % 2, r, :], s_buf[:, h % 2, r, :], inv_sum[:, h, r:r + 1],
                                                None, ALU.mult)
                    ins.then_inc(p_ready, 1)
                if h == 0:
                    split(Q2_ + tile_ahead(0) + AHEAD)
                if h == H0 - 2:
                    split(O0 + RING - 1)
            out_lo(H0 - 1)
            for g in range(O0 + RING, DOWN):
                split(g)

            def residual(r, done):
                for c in range(2):
                    eng.wait_ge(done, 2 * r + c + 1)
                    s = slice(512 * c, 512 * c + 512)
                    link(eng.tensor_tensor(xn[:, r, s], bank[2 * r + c], xn[:, r, s], ALU.add))
                    ins = eng.bn_stats(stats[:, r, c, :], xn[:, r, s])
                link(ins)
                link(eng.bn_aggr(mv[:, r, :], stats[:, r, :, :]))

            eng.wait_ge(xb_ready, 1)
            for r in range(NT):
                residual(r, out0_done)
                link(eng.tensor_scalar(st1[:, r, 0:1], mv[:, r, 1:2], EPS_LN, None, ALU.add))
                eng.scalar_tensor_tensor(out=st1[:, r, 1:2], in0=st1[:, r, 0:1], scalar=EPS_RMS, in1=mv[:, r, 1:2],
                                         op0=ALU.mult, op1=ALU.add).then_inc(var_ready, 1)
                eng.wait_ge(std_ready, r + 1)
                link(eng.reciprocal(st1[:, r, 4:6], st1[:, r, 2:4]))
                eng.tensor_scalar(xs[:, r, :], xn[:, r, :], mv[:, r, 0:1], st1[:, r, 5:6], ALU.subtract, ALU.mult) \
                   .then_inc(xs_ready, 1)
            split(DOWN)
            split(DOWN + 1)

            def onehots(g):
                if g >= EG:
                    return
                if g >= 2:
                    eng.wait_ge(msg_done, GT * g)
                for s, row in enumerate((src_row, dst_row)):
                    for r in range(NT):
                        ins = eng.tensor_scalar(onehot[:, g % 2, NT * s + r, :], row[:, GT * P * g:GT * P * (g + 1)],
                                                node_id[:, r:r + 1], None, ALU.is_equal)
                ins.then_inc(onehot_ready, 1)

            for n, ft in enumerate(FT_ORDER):
                eng.wait_ge(b_hi_ready, n + 1)
                eng.scalar_tensor_tensor(out=b_lo[:, ft, :], in0=bank[ft][:, 0:N], scalar=colv[:, RMSW, ft:ft + 1],
                                         in1=b_hi[:, ft, :].bitcast(F32), op0=ALU.mult, op1=ALU.subtract) \
                   .then_inc(b_lo_ready, 1)
            split(LR)
            for f in range(2):
                eng.wait_ge(evac_hi, evac_number(DOWN + f) + 1)
                eng.tensor_tensor(h_lo[:, f, :], bank[6 + f][:, 0:N], h_hi[:, f, :].bitcast(F32),
                                  ALU.subtract).then_inc(evac_lo, 1)
            eng.tensor_copy(ident_r[:], ident[:]).then_inc(ident_ready, 1)
            eng.wait_ge(att_loaded, 16)
            for r in range(NT):
                eng.wait_ge(lr_hi_ready, 2 * r + 1)
                link(eng.tensor_tensor(za_buf[:, 0, 0:2, :], bank[2 + r].rearrange("p (s f) -> p s f", s=2),
                                       att_row[:].unsqueeze(1).to_broadcast([P, 2, HID]), ALU.mult))
                eng.tensor_reduce(g_att[:, r, :], za_buf[:, 0, 0:2, :].rearrange("p s (h d) -> p (s h) d", h=H1),
                                  AX.X, ALU.add).then_inc(g_ready, 1)
                eng.wait_ge(lr_hi_ready, 2 * r + 2)
                eng.tensor_tensor(lr_lo[:, r, :, 0:HID], bank[2 + r].rearrange("p (s f) -> p s f", s=2),
                                  lr_hi[:, r, :, 0:HID].bitcast(F32), ALU.subtract)
                eng.tensor_tensor(lr_lo[:, r, :, HID:HG], g_att[:, r, :].rearrange("p (s h) -> p s h", s=2),
                                  lr_hi[:, r, :, HID:HG].bitcast(F32), ALU.subtract).then_inc(lr_lo_ready, 1)
            eng.wait_ge(rows_loaded, 32)
            onehots(0)
            onehots(1)
            split(UP)
            split(UP + 1)
            for r in range(NT):
                eng.tensor_scalar(xn[:, r, :], xn[:, r, :], mv[:, r, 0:1], st1[:, r, 4:5], ALU.subtract, ALU.mult)
            for g in range(EG + 1):
                if g >= 1:
                    onehots(g + 1)
                eng.wait_ge(z_ready, GT * (g + 1))
                ins = eng.tensor_tensor(za_buf[:, g % 2, :, :], z_buf[:, g % 2, :, :],
                                        att_row[:].unsqueeze(1).to_broadcast([P, GT, HID]), ALU.mult)
                ins.then_inc(z_used, 1)
                eng.wait_ge(z_used, g + 1)
                link(eng.tensor_reduce(score_e[:, GT * g:GT * g + GT, :],
                                       za_buf[:, g % 2, :, :].rearrange("p t (h d) -> p t h d", h=H1), AX.X, ALU.add))
                eng.scalar_tensor_tensor(out=score_e[:, GT * g:GT * g + GT, :],
                                         in0=psum[:, GT * (g % 2):GT * (g % 2) + GT, HID:HG], scalar=SLOPE,
                                         in1=score_e[:, GT * g:GT * g + GT, :], op0=ALU.mult, op1=ALU.add) \
                   .then_inc(score_ready, 1)
            def maxima1(r):
                eng.wait_ge(scores_loaded[r], 32)
                link(eng.tensor_tensor(sc0[:, r, :], sc0[:, r, :], sc1[:, r, :], ALU.max))
                link(eng.tensor_reduce(m1[:, r, 0, :], sc0[:, r, :].rearrange("p (s h) -> p h s", h=H1), AX.X, ALU.max))
                eng.tensor_scalar(m1[:, r, 1, :], m1[:, r, 0, :], -1.0, None, ALU.mult).then_inc(max1_ready, 1)

            def sums1(r):
                for h in range(H1):
                    eng.wait_ge(exp1_done, H1 * r + h + 1)
                    ins = eng.tensor_tensor_reduce(p1[:, r, h, :], p1[:, r, h, :], count[:, r, :], 1.0, 0.0,
                                                   ALU.mult, ALU.add, m1[:, r, 2, h:h + 1])
                link(ins)
                link(eng.tensor_scalar(m1[:, r, 2, :], m1[:, r, 2, :], EPS_DEN, None, ALU.add))
                eng.reciprocal(m1[:, r, 3, :], m1[:, r, 2, :]).then_inc(sum1_ready, 1)

            eng.wait_ge(count_loaded, 16)
            maxima1(0)
            maxima1(1)
            sums1(0)
            maxima1(2)
            sums1(1)
            sums1(2)
            for h in range(H1 + 1):
                if h < H1:
                    for i in range(NT):
                        c = NT * h + i
                        eng.wait_ge(at_hi_ready, c + 1)
                        eng.tensor_tensor(at_lo[:, h % 2, i, :], bank[c % 4][:, 0:N], at_hi[:, h % 2, i, :].bitcast(F32),
                                          ALU.subtract).then_inc(at_lo_ready, 1)
                if h >= 1:
                    k = h - 1
                    eng.wait_ge(o2_hi_ready, k + 1)
                    eng.tensor_tensor(o2_lo[rows(k), k // 2, :], bank[6 + k % 2][rows(k), 0:N],
                                      o2_hi[rows(k), k // 2, :].bitcast(F32), ALU.subtract).then_inc(o2_lo_ready, 1)
            for r in range(NT):
                residual(r, up_done)
                eng.tensor_scalar(st1[:, r, 0:1], mv[:, r, 1:2], EPS_LN, None, ALU.add).then_inc(var_ready, 1)
                eng.wait_ge(std_ready, NT + r + 1)
                link(eng.reciprocal(st1[:, r, 4:5], st1[:, r, 2:3]))
                eng.tensor_scalar(xn[:, r, :], xn[:, r, :], mv[:, r, 0:1], st1[:, r, 4:5], ALU.subtract,
                                  ALU.mult).then_inc(x2_ready, 1)

        @block.tensor
        def _(eng):
            def product(dst, a, b, start, stop):
                eng.matmul(dst, a[0], b[0], start=start, stop=False)
                eng.matmul(dst, a[0], b[1], start=False, stop=False)
                return eng.matmul(dst, a[1], b[0], start=False, stop=stop)

            def chunk(g, f):
                return w_hi[:, g % RING, f], w_lo[:, g % RING, f]

            def wait_chunk(g):
                eng.wait_ge(w_hi_ready, g + 1)
                eng.wait_ge(w_lo_ready, g + 1)

            def free_bank(g):
                n = evac_number(g)
                if n >= 2:
                    eng.wait_ge(evac_lo, n - 1)

            def project(g, src, kts, inputs_evac=None):
                b = bank[evac_number(g) % 2][:, 0:N]
                for kt in kts:
                    if inputs_evac is not None:
                        eng.wait_ge(evac_lo, inputs_evac + kt + 1)
                    mm = product(b, chunk(g, slice(kt * P, kt * P + P)), (src[0][:, kt, :], src[1][:, kt, :]),
                                 kt == 0, kt == FT - 1)
                if kts[-1] == FT - 1:
                    mm.then_inc(proj_done, 1)

            def keyrows(j):
                if j >= EG:
                    return
                if j >= 2:
                    eng.wait_ge(idx_ready, j - 1)
                for i in range(GT):
                    t = GT * j + i
                    mm = eng.matmul(bank[6 + j % 2][:, P * i:P * i + P], key0[:, t:t + 1].to_broadcast([P, P]), ident[:],
                                    start=True, stop=True)
                mm.then_inc(keyrow_ready, 1)

            every = list(range(FT))
            for g in range(V0, V2_):
                wait_chunk(g)
                free_bank(g)
                if g == V0:
                    for c in range(2):
                        eng.wait_ge(xlo_ready, c + 1)
                        project(g, (xT_hi, xT_lo), every[4 * c:4 * c + 4])
                    eng.wait_ge(keys_ready, 1)
                    eng.wait_ge(consts, 1)
                    keyrows(0)
                else:
                    project(g, (xT_hi, xT_lo), every)
                keyrows(g - V0 + 1)
            eng.wait_ge(evac_lo, FT)
            for g in range(V2_, K0):
                kt = g - V2_
                wait_chunk(g)
                for r in range(NT):
                    a = (a_hi[:, kt, r * P:r * P + P], a_lo[:, kt, r * P:r * P + P])
                    for c in range(2):
                        mm = product(bank[2 * r + c], a, chunk(g, slice(512 * c, 512 * c + 512)), kt == 0, kt == FT - 1)
                mm.then_inc(v2_done, 1)
                keyrows(g - V0 + 1)
            for g in range(K0, K2_):
                wait_chunk(g)
                if g < K0 + 2:
                    eng.wait_ge(v2_sum, g - K0 + 1)
                else:
                    free_bank(g)
                project(g, (xT_hi, xT_lo), every)
            for g in range(K2_, Q0):
                wait_chunk(g)
                free_bank(g)
                project(g, (a_hi, a_lo), every, evac_number(K0) if g == K2_ else None)
            for g in range(Q0, Q2_):
                wait_chunk(g)
                free_bank(g)
                project(g, (xT_hi, xT_lo), every)
            wait_chunk(Q2_)
            free_bank(Q2_)
            project(Q2_, (a_hi, a_lo), every, evac_number(Q0))
            eng.wait_ge(v2_lo_ready, 6)
            eng.wait_ge(idx_ready, EG)
            def scores(h):
                t = h // 2
                eng.wait_ge(evac_lo, evac_number(Q2_) + t + 1)
                for r in range(NT):
                    if h >= 1:
                        eng.wait_ge(s_ready, NT * (h - 1) + r + 1)
                    q = (q2_hi[rows(h), t % 2, r * P:r * P + P], q2_lo[rows(h), t % 2, r * P:r * P + P])
                    product(bank[2 + r][:, 0:N], q, (k2_hi[rows(h), t, :], k2_lo[rows(h), t, :]), True, True) \
                        .then_inc(qk_done, 1)

            def turn(k, i):
                c = NT * k + i
                if i == 0:
                    eng.wait_ge(p_ready, k + 1)
                if c >= 2:
                    eng.wait_ge(pt_lo_ready, c - 1)
                for r in range(NT):
                    mm = eng.transpose(bank[5 + c % 2][:, r * P:r * P + P], s_buf[:, k % 2, r, i * P:i * P + P], ident[:])
                mm.then_inc(t_done, 1)

            def weigh(k):
                if k >= 1:
                    eng.wait_ge(oT_lo_ready, k)
                c = slice(k // 2 * P, k // 2 * P + P)
                for i in range(NT):
                    eng.wait_ge(pt_lo_ready, NT * k + i + 1)
                    mm = product(bank[7][:, 0:N], (v2_hi[:, i, c], v2_lo[:, i, c]),
                                 (pt_hi[:, k % 2, i, :], pt_lo[:, k % 2, i, :]), i == 0, i == NT - 1)
                mm.then_inc(av_done, 1)

            def output_part(kt, r, halves=range(2)):
                a = (oT_hi[:, kt, r * P:r * P + P], oT_lo[:, kt, r * P:r * P + P])
                for c in halves:
                    mm = product(bank[2 * r + c], a, chunk(O0 + kt, slice(512 * c, 512 * c + 512)), kt == 0, kt == FT - 1)
                return mm

            for h in range(H0 + 1):
                if h >= 1:
                    turn(h - 1, 0)
                    turn(h - 1, 1)
                if h < H0:
                    scores(h)
                if h >= 1:
                    turn(h - 1, 2)
                if h == 0:
                    wait_chunk(Q2_ + 1)
                    free_bank(Q2_ + 1)
                    project(Q2_ + 1, (a_hi, a_lo), every)
                elif 2 <= h < H0 - 2:
                    t = h // 2 + 1
                    if h % 2 == 0:
                        wait_chunk(Q2_ + t)
                        free_bank(Q2_ + t)
                    project(Q2_ + t, (a_hi, a_lo), every[4 * (h % 2):4 * (h % 2) + 4])
                if h >= 1:
                    weigh(h - 1)
                if h == H0 - 1:
                    for kt in range(RING):
                        wait_chunk(O0 + kt)
                        output_part(kt, 0)
            for kt in range(RING):
                for r in range(1, NT):
                    mm = output_part(kt, r)
                mm.then_inc(out0_part, 1)
            for r in range(NT):
                for c in range(2):
                    for kt in range(RING, FT):
                        if r == 0 and c == 0:
                            wait_chunk(O0 + kt)
                            eng.wait_ge(oT_lo_ready, 2 * kt + 2)
                        mm = output_part(kt, r, [c])
                    mm.then_inc(out0_done, 1)
            for ready, tiles in ((1, [(0, 6), (0, 7), (0, 0), (0, 1)]),
                                 (2, [(1, 6), (1, 7), (1, 0), (1, 1), (0, 2), (1, 2), (0, 3), (1, 3)]),
                                 (3, [(0, 4), (1, 4), (0, 5), (1, 5)] + [(2, ft) for ft in FT_ORDER])):
                eng.wait_ge(xs_ready, ready)
                for r, ft in tiles:
                    mm = eng.transpose(bank[ft][:, r * P:r * P + P], xs[:, r, ft * P:ft * P + P], ident[:])
                    if r == NT - 1:
                        mm.then_inc(bt_done, 1)
            wait_chunk(DOWN)
            wait_chunk(DOWN + 1)
            for n, kt in enumerate(FT_ORDER):
                for f in range(2):
                    eng.wait_ge(b_lo_ready, min(n + 1 + f, FT))
                    mm = product(bank[6 + f][:, 0:N], chunk(DOWN + f, slice(kt * P, kt * P + P)),
                                 (b_hi[:, kt, :], b_lo[:, kt, :]), n == 0, n == FT - 1)
                    if n == FT - 1:
                        mm.then_inc(proj_done, 1)
            wait_chunk(LR)
            eng.wait_ge(b_lo_ready, FT)
            for r in range(NT):
                for f in range(2):
                    eng.wait_ge(evac_lo, evac_number(DOWN) + f + 1)
                    mm = product(bank[2 + r], (h_hi[:, f, r * P:r * P + P], h_lo[:, f, r * P:r * P + P]),
                                 chunk(LR, slice(512 * f, 512 * f + 512)), f == 0, f == 1)
                mm.then_inc(lr_done, 1)
            eng.wait_ge(ident_ready, 1)
            for g in range(EG + 1):
                if g >= 1:
                    eng.wait_ge(onehot_ready, g)
                for i in range(GT):
                    if g == 0:
                        eng.wait_ge(lr_lo_ready, i + 1)
                    if g >= 2:
                        eng.wait_ge(score_ready, g - 1)
                    b = bank[GT * (g % 2) + i][:, 0:HG]
                    if g == 0:
                        parts = [(ident_r[:], s, i) for s in range(2)]
                        eng.wait_ge(lr_lo_ready, NT)
                    else:
                        parts = [(onehot[:, (g - 1) % 2, NT * s + r, i * P:i * P + P], s, r)
                                 for s in range(2) for r in range(NT)]
                    for n, (hot, s, r) in enumerate(parts):
                        eng.matmul(b, hot, lr_hi[:, r, s, :], start=(n == 0), stop=False)
                        mm = eng.matmul(b, hot, lr_lo[:, r, s, :], start=False, stop=(n == len(parts) - 1))
                    mm.then_inc(msg_done, 1)
            for h in range(H1 + 1):
                if h < H1:
                    eng.wait_ge(p1_ready, H1 * (NT - 1) + h + 1)
                    for i in range(NT):
                        c = NT * h + i
                        if c >= 4:
                            eng.wait_ge(at_lo_ready, c - 3)
                        for r in range(NT):
                            mm = eng.transpose(bank[c % 4][:, r * P:r * P + P], p1[:, r, h, i * P:i * P + P], ident[:])
                        mm.then_inc(t1_done, 1)
                if h >= 1:
                    k = h - 1
                    if k >= 2:
                        eng.wait_ge(o2_lo_ready, k - 1)
                    c = slice(k // 2 * P, k // 2 * P + P)
                    for i in range(NT):
                        eng.wait_ge(at_lo_ready, NT * k + i + 1)
                        mm = product(bank[6 + k % 2][:, 0:N], (lr_hi[:, i, 0, c], lr_lo[:, i, 0, c]),
                                     (at_hi[:, k % 2, i, :], at_lo[:, k % 2, i, :]), i == 0, i == NT - 1)
                    mm.then_inc(av1_done, 1)
            wait_chunk(UP + 1)
            eng.wait_ge(o2_lo_ready, H1)
            for r in range(NT):
                for c in range(2):
                    for f in range(2):
                        mm = product(bank[2 * r + c], (o2_hi[:, f, r * P:r * P + P], o2_lo[:, f, r * P:r * P + P]),
                                     chunk(UP + f, slice(512 * c, 512 * c + 512)), f == 0, f == 1)
                    mm.then_inc(up_done, 1)


def kernel(**inputs):
    import concourse.bacc as bacc
    from concourse.bass_utils import run_bass_kernel_spmd

    a = {k: np.asarray(v) for k, v in inputs.items()}

    def by_out_tile(wT):
        i, o = wT.shape
        return wT.reshape(i // P, P, o // P, P).transpose(2, 1, 0, 3).reshape(o // P, P, -1)

    def by_in_tile(wT):
        return wT.reshape(wT.shape[0] // P, P, -1)

    g0 = {k[7:]: v for k, v in a.items() if k.startswith("L0_gnn_")}
    g1 = {k[7:]: v for k, v in a.items() if k.startswith("L1_gnn_")}
    lr = np.concatenate([g1["Wl"], g1["Wr"]], axis=1)
    w_stream = np.concatenate([
        by_out_tile(g0["wv"].T), by_in_tile(g0["wiv"].T), by_out_tile(g0["wk"].T), by_out_tile(g0["wik"].T),
        by_out_tile(g0["wq"].T), by_out_tile(g0["wiq"].T), by_in_tile(g0["wo"].T), by_out_tile(g1["W_down"]),
        lr.reshape(2, P, 2 * HID).transpose(1, 0, 2).reshape(1, P, -1), by_in_tile(g1["W_up"]),
    ])
    vectors = [g0["bq"], g0["bk"], g0["bv"], g0["biq"], g0["bik"], g1["rms_w"]]
    arrays = {
        "w_stream": w_stream,
        "xT": a["x"].T.reshape(FT, P, N).transpose(1, 0, 2),
        "x": a["x"],
        "cols": np.stack([v.reshape(FT, P).T for v in vectors], axis=1),
        "biv": g0["biv"], "bo": g0["bo"], "etw": g0["edge_type_weights"], "att": g1["att"].reshape(-1),
        "srcP": a["src"][:E].reshape(ET, P).T, "dstP": a["dst"][:E].reshape(ET, P).T,
        "typP": a["edge_type_5"].reshape(ET, P).T, "srcL": a["src"], "dstL": a["dst"],
    }
    arrays = {k: np.ascontiguousarray(v) for k, v in arrays.items()}
    nc = bacc.Bacc("TRN2", target_bir_lowering=False, num_devices=1)
    args = [nc.dram_tensor(f"in_{k}", v.shape, mybir.dt.from_np(v.dtype), kind="ExternalInput").ap()
            for k, v in arrays.items()]
    out = nc.dram_tensor("out_x", (N, F), F32, kind="ExternalOutput").ap()
    gnn(nc, *args, out)
    got = run_bass_kernel_spmd(nc, [{f"in_{k}": v for k, v in arrays.items()}], core_ids=[0])
    return got.results[0]["out_x"]
```
